# Optimizing a Trainium2 kernel written in Bass

```python
import numpy as np
import jax
import jax.numpy as jnp

def _softmax(x, axis=-1):
    return jax.nn.softmax(x, axis=axis)
def _gelu(x):
    return jax.nn.gelu(x, approximate=True)
def _silu(x):
    return jax.nn.silu(x)
def _sigmoid(x):
    return jax.nn.sigmoid(x)
def _layernorm(x, axis=-1, eps=1e-5):
    m = jnp.mean(x, axis=axis, keepdims=True)
    v = jnp.var(x, axis=axis, keepdims=True)
    return (x - m) / jnp.sqrt(v + eps)
def _scatter_add(tgt, idx, src, axis=0):
    return tgt.at[idx].add(src)
def _segment_sum(src, seg, n):
    return jax.ops.segment_sum(src, seg, n)

kernel_name = 'mk_conv_seq_d1_conv_nhwc512_2b4920'

def setup_inputs(seed: int = 0):
    np.random.seed(seed)
    _w = jnp.asarray
    def _rec_inputs():
        import jax
        import jax.numpy as jnp
        _gk = jax.random.key(seed)
        x = -0.0002928 + 1 * jax.random.normal(jax.random.fold_in(_gk, 1), (512, 4, 4, 512), jnp.float32)
        return x
    x = _rec_inputs()
    def _L0_conv_setup():
        import jax, jax.numpy as jnp
        import numpy as np
        import math
        NH = 8
        EPS = 1e-05

        def _pe(S, D):
            pos = jnp.arange(S, dtype=jnp.float32)[:, None]
            div = jnp.exp(jnp.arange(0, D, 2, dtype=jnp.float32) * (-math.log(10000.0) / D))
            ang = pos * div
            pe = jnp.zeros((S, D), jnp.float32)
            pe = pe.at[:, 0::2].set(jnp.sin(ang)).at[:, 1::2].set(jnp.cos(ang))
            return pe

        def _ln(x, g, b):
            m = x.mean(-1, keepdims=True)
            v = ((x - m) ** 2).mean(-1, keepdims=True)
            return (x - m) / jnp.sqrt(v + EPS) * g + b
        key = jax.random.key(seed)
        ks = jax.random.split(key, 6)
        S, H, W, D, dff = (512, 4, 4, 512, 2048)
        x = jax.random.normal(ks[0], (S, H, W, D), jnp.float32)
        s = 1.0 / math.sqrt(D)
        Wq = jax.random.normal(ks[1], (D, D), jnp.float32) * s
        Wfc = jax.random.normal(ks[2], (D, D), jnp.float32) * s
        W1 = jax.random.normal(ks[3], (dff, D), jnp.float32) * s
        b1 = jnp.zeros((dff,), jnp.float32)
        W2 = jax.random.normal(ks[4], (D, dff), jnp.float32) * (1.0 / math.sqrt(dff))
        b2 = jnp.zeros((D,), jnp.float32)
        g1 = jnp.ones((D,), jnp.float32)
        be1 = jnp.zeros((D,), jnp.float32)
        g2 = jnp.ones((D,), jnp.float32)
        be2 = jnp.zeros((D,), jnp.float32)
        return dict(x=x, Wq=Wq, Wfc=Wfc, W1=W1, b1=b1, W2=W2, b2=b2, g1=g1, be1=be1, g2=g2, be2=be2)
    _L0_conv_all = _L0_conv_setup()
    _L0_conv_in = {k: v for k, v in _L0_conv_all.items() if k in ('Wq', 'Wfc', 'W1', 'b1', 'W2', 'b2', 'g1', 'be1', 'g2', 'be2', )}
    del _L0_conv_all

    return {
        "x": x,
        "L0_conv_Wq": _L0_conv_in["Wq"],
        "L0_conv_Wfc": _L0_conv_in["Wfc"],
        "L0_conv_W1": _L0_conv_in["W1"],
        "L0_conv_b1": _L0_conv_in["b1"],
        "L0_conv_W2": _L0_conv_in["W2"],
        "L0_conv_b2": _L0_conv_in["b2"],
        "L0_conv_g1": _L0_conv_in["g1"],
        "L0_conv_be1": _L0_conv_in["be1"],
        "L0_conv_g2": _L0_conv_in["g2"],
        "L0_conv_be2": _L0_conv_in["be2"],
    }

def reference(x, L0_conv_Wq, L0_conv_Wfc, L0_conv_W1, L0_conv_b1, L0_conv_W2, L0_conv_b2, L0_conv_g1, L0_conv_be1, L0_conv_g2, L0_conv_be2):
    import jax
    import jax.numpy as jnp
    def _L0_conv_ref(x, Wq, Wfc, W1, b1, W2, b2, g1, be1, g2, be2):
        import jax, jax.numpy as jnp
        import numpy as np
        import math
        NH = 8
        EPS = 1e-05

        def _pe(S, D):
            pos = jnp.arange(S, dtype=jnp.float32)[:, None]
            div = jnp.exp(jnp.arange(0, D, 2, dtype=jnp.float32) * (-math.log(10000.0) / D))
            ang = pos * div
            pe = jnp.zeros((S, D), jnp.float32)
            pe = pe.at[:, 0::2].set(jnp.sin(ang)).at[:, 1::2].set(jnp.cos(ang))
            return pe

        def _ln(x, g, b):
            m = x.mean(-1, keepdims=True)
            v = ((x - m) ** 2).mean(-1, keepdims=True)
            return (x - m) / jnp.sqrt(v + EPS) * g + b
        S, H, Wd, D = x.shape
        depth = D // NH
        q = x @ Wq.T + _pe(S, D)[:, None, None, :]
        q5 = jnp.swapaxes(q.reshape(H, Wd, S, NH, depth), 2, 3)
        k_t = jnp.swapaxes(q5, 3, 4)
        scale = 1.0 / math.sqrt(depth)
        bmm_qk = jnp.einsum('hwink,hwijm->hwinm', q5 * scale, k_t)
        qk = jax.nn.softmax(bmm_qk, axis=-1)
        qk = jnp.einsum('hwink,hwijm->hwinm', qk, k_t)
        attn_weights = jax.nn.softmax(qk, axis=-1)
        out = jnp.einsum('hwijk,hwikn->hwijn', attn_weights, q5)
        attn_out = out.reshape(S, H, Wd, NH * depth) @ Wfc.T
        o1 = _ln(x + attn_out, g1, be1)
        ffn = jax.nn.relu(o1 @ W1.T + b1) @ W2.T + b2
        return _ln(o1 + ffn, g2, be2)

    def _gn(v, G=32, eps=1e-5):
        B_, H_, W_, C_ = v.shape
        g = v.reshape(B_, H_, W_, G, C_ // G)
        m = jnp.mean(g, axis=(1, 2, 4), keepdims=True)
        s = jnp.var(g, axis=(1, 2, 4), keepdims=True)
        return ((g - m) / jnp.sqrt(s + eps)).reshape(v.shape)

    def _ln_c(v, eps=1e-6):
        m = jnp.mean(v, axis=-1, keepdims=True)
        s = jnp.var(v, axis=-1, keepdims=True)
        return (v - m) / jnp.sqrt(s + eps)

    def _ln_t(v, eps=1e-5):
        m = jnp.mean(v, axis=-1, keepdims=True)
        s = jnp.var(v, axis=-1, keepdims=True)
        return (v - m) / jnp.sqrt(s + eps)

    def _to_tokens(v):
        B_, H_, W_, C_ = v.shape
        return v.reshape(B_, H_ * W_, C_)
    def _from_tokens(t, like):
        return t.reshape(like.shape)

    x = _L0_conv_ref(x, L0_conv_Wq, L0_conv_Wfc, L0_conv_W1, L0_conv_b1, L0_conv_W2, L0_conv_b2, L0_conv_g1, L0_conv_be1, L0_conv_g2, L0_conv_be2)
    return x


_drawn_inputs = setup_inputs


def setup_inputs(seed=0):
    import zlib

    import numpy as np

    out = dict(_drawn_inputs(seed))
    spreads = {'L0_conv_b1': (0.0, 0.1),
     'L0_conv_b2': (0.0, 0.1),
     'L0_conv_g1': (1.0, 0.2),
     'L0_conv_be1': (0.0, 0.1),
     'L0_conv_g2': (1.0, 0.2),
     'L0_conv_be2': (0.0, 0.1)}
    factors = {}
    for name, (base, spread) in spreads.items():
        noise = np.random.default_rng([zlib.crc32(name.encode()), seed]).standard_normal(out[name].shape)
        drawn = base * np.exp(spread * noise) if base else spread * noise
        out[name] = jnp.asarray(drawn.astype(out[name].dtype))
    for name, factor in factors.items():
        out[name] = (out[name] * factor).astype(out[name].dtype)
    return out
```

```python
import concourse.bass as bass
from concourse import mybir
from contextlib import ExitStack

D = 512
DFF = 2048
NH = 8
DEPTH = D // NH
TB = 512
NB = 16
P = 128
NT = TB // P
NC = D // P
NJ = DFF // P
SPB = TB // 16
EPS = 1e-5


def conv_seq_kernel(nc, x, wq, wqT, wfcT, w1T, b1, w2T, b2, g1, be1, g2, be2, pe, pe_r, masks, out):
    f32 = mybir.dt.float32
    f16 = mybir.dt.float16
    u32 = mybir.dt.uint32
    ALU = mybir.AluOpType
    ACT = mybir.ActivationFunctionType
    AX = mybir.AxisListType

    x_v = x.rearrange("(b p t) f -> b p (t f)", p=P, t=NT)
    out_v = out.rearrange("(b p t) f -> b p (t f)", p=P, t=NT)
    pe_v = pe.rearrange("(b s) f -> b s f", s=SPB)
    w1_v = w1T.rearrange("(c p) (q n) -> q p c n", p=P, q=4)
    w2_v = w2T.rearrange("(q j p) n -> q p j n", p=P, q=4)

    ctx = ExitStack()
    with ctx:
        def sb(name, shape, dt=f32):
            return ctx.enter_context(nc.sbuf_tensor(name, shape, dt))

        def pb(name):
            return ctx.enter_context(nc.psum_tensor(name, [P, 512], f32))

        def sem(name):
            return ctx.enter_context(nc.semaphore(name))

        w1hi = sb("w1hi", [P, NC, DFF], f16)
        w1lo = sb("w1lo", [P, NC, DFF], f16)
        w2 = sb("w2", [P, 2, NJ, D], f16)
        w2hi, w2lo = w2[:, 0], w2[:, 1]
        wqT_sb = sb("wqT_sb", [P, NC, D])
        wrB = sb("wrB", [P, NH, D])
        wfcS = sb("wfcS", [P, D])
        g1B = sb("g1B", [P, D])
        addB = sb("addB", [P, D])
        g2B = sb("g2B", [P, D])
        be2B = sb("be2B", [P, D])
        masks_sb = sb("masks_sb", [P, 3 * P + SPB])
        ident = masks_sb[:, 0:P]
        fold = masks_sb[:, P:2 * P]
        ones = masks_sb[:, 2 * P:3 * P]
        ind = masks_sb[:, 3 * P:3 * P + SPB]
        peR = sb("peR", [P, NB, NH])
        cols = sb("cols", [P, NJ + 2 * NC])
        colsS = sb("colsS", [P, NJ + 2 * NC])
        b1S = colsS[:, 0:NJ]
        g1S = colsS[:, NJ:NJ + NC]
        be1S = colsS[:, NJ + NC:NJ + 2 * NC]
        xb = sb("xb", [P, 2, NT, D])
        peb = sb("peb", [SPB, 2, D])
        yz = sb("yz", [P, NT, D])
        o1b = sb("o1b", [P, 2, NT, D])
        y2 = sb("y2", [P, NT, D])
        o1f = sb("o1f", [P, 2, TB])
        o1hi = sb("o1hi", [P, 2, NC, TB], f16)
        o1lo = sb("o1lo", [P, 2, NC, TB], f16)
        hf = sb("hf", [P, 2, TB])
        hhi = sb("hhi", [P, 2, TB], f16)
        hlo = sb("hlo", [P, 2, TB], f16)
        scr = sb("scr", [P, 2, D])
        rr = sb("rr", [P, NT, NH])
        rp = sb("rp", [P, NT, NH])
        rs = sb("rs", [P, NT, NH])
        ee = sb("ee", [P, 2, NT, NH])
        es = sb("es", [P, 2, NH])
        rmx = sb("rmx", [P, NH])
        mxB = sb("mxB", [P, NH])
        xbT = sb("xbT", [P, NC, NH])
        zT = sb("zT", [SPB, NH])
        rden = sb("rden", [P, NH])
        ocx = sb("ocx", [P, NH, 16])
        bn = sb("bn", [P, 2, NT, 6])
        mv = sb("mv", [P, 2, NT, 2])
        var_eps = sb("var_eps", [P, 2, NT])
        rstd = sb("rstd", [P, 2, NT])
        nmr = sb("nmr", [P, 2, NT])
        half = sb("half", [P, NT])
        wmx = sb("wmx", [P, 16])
        amx = sb("amx", [P, 4])
        amxB = sb("amxB", [P, 4])
        bnd = sb("bnd", [P, 8])
        pw = sb("pw", [P, 4])
        sc = sb("sc", [P, 4])
        isc = sb("isc", [P, 4])
        cc = sb("cc", [P, 4])
        c1 = cc[:, 1:2]
        c2 = cc[:, 2:3]

        w1_st = w2[:, :, :, :].rearrange("p a j n -> p (a j n)").bitcast(f32).rearrange(
            "p (q c n) -> p q c n", q=4, c=NC)
        wq_st = y2
        wfc_st = o1b[:, 1]
        w2_st = [y2[:, :, :], o1b[:, 1]]
        be1_st = o1f[:, 0, :]
        b2_st = o1f[:, 1, :]

        acc = [pb(f"acc{t}") for t in range(NT)]
        hps = [pb(f"hps{t}") for t in range(2)]
        aux = [pb(f"aux{t}") for t in range(2)]

        dma_x = [sem("dma_x0"), sem("dma_x1")]
        dma_small, dma_wq, dma_wqT, dma_wfc = sem("dma_small"), sem("dma_wq"), sem("dma_wqT"), sem("dma_wfc")
        dma_w1 = [sem(f"dma_w1_{q}") for q in range(4)]
        dma_w2 = [sem(f"dma_w2_{q}") for q in range(2)]
        dma_out = sem("dma_out")
        wr_ready, wrB_ready, wfc_ready, wfcS_ready = sem("wr_ready"), sem("wrB_ready"), sem("wfc_ready"), sem("wfcS_ready")
        consts_set = sem("consts_set")
        w1_max, w2_max, small_max, max_all, max2_all = sem("w1_max"), sem("w2_max"), sem("small_max"), sem("max_all"), sem("max2_all")
        bound_ready, scale_step, scales_ready = sem("bound_ready"), sem("scale_step"), sem("scales_ready")
        w2_scale = sem("w2_scale")
        w1hi_ready, w1lo_ready, w2hi_ready, w2lo_ready = sem("w1hi_ready"), sem("w1lo_ready"), sem("w2hi_ready"), sem("w2lo_ready")
        addB_ready = sem("addB_ready")
        ffn1_done, ffn2_done = sem("ffn1_done"), sem("ffn2_done")
        hhi_ready, hf_ready, hlo_ready = sem("hhi_ready"), sem("hf_ready"), sem("hlo_ready")
        r_ready, rp_ready, rmx_ready, mx_ready, rs_ready = sem("r_ready"), sem("rp_ready"), sem("rmx_ready"), sem("mx_ready"), sem("rs_ready")
        e_ready, es_ready = sem("e_ready"), sem("es_ready")
        xbar_done, xbar_copied, o_done, ocx_ready, ao_done = sem("xbar_done"), sem("xbar_copied"), sem("o_done"), sem("ocx_ready"), sem("ao_done")
        y_ready, bn_ready, mv_ready, z_ready, zT_done = sem("y_ready"), sem("bn_ready"), sem("mv_ready"), sem("z_ready"), sem("zT_done")
        var_ready, rstd_ready = sem("var_ready"), sem("rstd_ready")
        o1hi_ready, o1f_ready, o1lo_ready = sem("o1hi_ready"), sem("o1f_ready"), sem("o1lo_ready")
        o1g_ready, o1b_ready = sem("o1g_ready"), sem("o1b_ready")
        y2_ready, bn2_ready, mv2_ready = sem("y2_ready"), sem("bn2_ready"), sem("mv2_ready")
        ln2_step, z2_ready, z2g_ready, out_ready = sem("ln2_step"), sem("z2_ready"), sem("z2g_ready"), sem("out_ready")

        dve_passed, pool_passed = sem("dve_passed"), sem("pool_passed")

        block = ctx.enter_context(nc.Block())

        @block.sync
        def _(sp):
            def load_x(b, slot):
                sp.dma_start(xb[:, slot].rearrange("p t f -> p (t f)"), x_v[b]).then_inc(dma_x[slot], 16)
                sp.dma_start(peb[:, slot, :], pe_v[b]).then_inc(dma_x[slot], 16)

            sp.dma_start(wq_st[:, :, :], wq.rearrange("(c p) n -> p c n", p=P)).then_inc(dma_wq, 16)
            load_x(0, 0)
            for q in range(4):
                sp.dma_start(w1_st[:, q], w1_v[q]).then_inc(dma_w1[q], 16)
            load_x(1, 1)
            sp.wait_ge(wr_ready, NH)
            sp.wait_ge(wfc_ready, 1)
            for n in range(8):
                if 2 <= n < 6:
                    sp.wait_ge(w2_max, n - 1)
                if n >= 6:
                    sp.wait_ge(w2_max, 4)
                    sp.wait_ge(w2hi_ready, n - 5)
                    sp.wait_ge(w2lo_ready, n - 5)
                sp.dma_start(w2_st[n % 2], w2_v[n % 4]).then_inc(dma_w2[n % 2], 16)

            def next_x(n, slot):
                sp.wait_ge(y_ready, NT * (n - 1))
                load_x(n, slot)

            def store(b):
                sp.wait_ge(out_ready, NT * (b + 1))
                sp.dma_start(out_v[b], y2[:, :, :].rearrange("p t f -> p (t f)")).then_inc(dma_out, 16)

            next_x(2, 0)
            next_x(3, 1)
            with nc.sync.Fori(0, NB // 2 - 2) as i:
                for par in range(2):
                    store(2 * i + par)
                    next_x(2 * i + par + 4, par)
            for b in range(NB - 4, NB):
                store(b)
            sp.wait_ge(dma_out, 16 * NB)

        @block.gpsimd
        def _(pool):
            RMAX = bass.bass_isa.ReduceOp.max
            pool.memset(half[:, :], -0.5).then_inc(consts_set, 1)
            pool.memset(ocx[:, :, :], 0.0).then_inc(consts_set, 1)

            def passed():
                pool.sem_inc(pool_passed, 1)

            def token_max(n):
                pool.wait_ge(rmx_ready, n + 1)
                if not isinstance(n, int) or n > 0:
                    pool.wait_ge(rs_ready, n)
                passed()
                pool.partition_all_reduce(mxB[:, :], rmx[:, :], P, RMAX).then_inc(mx_ready, 1)

            def inv_std(k, mv_sem, n):
                pool.wait_ge(mv_sem, NT * (n + 1))
                passed()
                pool.tensor_scalar(var_eps[:, k], mv[:, k, :, 1], EPS, None, ALU.add).then_inc(var_ready, 1)

            def ln1(n, slot):
                inv_std(0, mv_ready, n)
                pool.wait_ge(var_ready, ln_count(n, 0) + 1)
                pool.tensor_tensor(rstd[:, 0], var_eps[:, 0], half[:, :], ALU.pow).then_inc(rstd_ready, 1)
                for t in range(NT):
                    pool.wait_ge(z_ready, NT * n + t + 1)
                    if t == 0 and (not isinstance(n, int) or n >= 2):
                        pool.wait_ge(y2_ready, NT * (n - 1))
                    if t == 0 and isinstance(n, int) and n == 0:
                        pool.wait_ge(addB_ready, 1)
                    pool.tensor_tensor(o1b[:, slot, t], yz[:, t], g1B[:, :], ALU.mult).then_inc(o1g_ready, 1)
                    pool.wait_ge(o1g_ready, NT * n + t + 1)
                    pool.tensor_tensor(o1b[:, slot, t], o1b[:, slot, t], addB[:, :], ALU.add).then_inc(o1b_ready, 1)

            def ln2(b):
                inv_std(1, mv2_ready, b)
                pool.wait_ge(var_ready, ln_count(b, 1) + 1)
                pool.tensor_tensor(rstd[:, 1], var_eps[:, 1], half[:, :], ALU.pow).then_inc(ln2_step, 1)
                pool.wait_ge(ln2_step, 3 * b + 1)
                pool.tensor_tensor(nmr[:, 1], mv[:, 1, :, 0], rstd[:, 1], ALU.mult).then_inc(ln2_step, 1)
                pool.wait_ge(ln2_step, 3 * b + 2)
                passed()
                pool.tensor_scalar(nmr[:, 1], nmr[:, 1], -1.0, None, ALU.mult).then_inc(ln2_step, 1)
                pool.wait_ge(ln2_step, 3 * b + 3)
                passed()
                for t in range(NT):
                    pool.tensor_scalar(y2[:, t], y2[:, t], rstd[:, 1, t:t + 1], nmr[:, 1, t:t + 1],
                                       ALU.mult, ALU.add).then_inc(z2_ready, 1)
                    pool.wait_ge(z2_ready, NT * b + t + 1)
                    pool.tensor_tensor(y2[:, t], y2[:, t], g2B[:, :], ALU.mult).then_inc(z2g_ready, 1)
                    pool.wait_ge(z2g_ready, NT * b + t + 1)
                    pool.tensor_tensor(y2[:, t], y2[:, t], be2B[:, :], ALU.add).then_inc(out_ready, 1)

            def ln_count(n, k):
                if k == 0:
                    return 2 * n - 1 if not isinstance(n, int) or n > 0 else 0
                return 2 * (n + 1) if not isinstance(n, int) or n < NB - 1 else 2 * n + 1

            pool.wait_ge(consts_set, 2)
            pool.wait_ge(w1_max, 5)
            pool.partition_all_reduce(amxB[:, 0:2], amx[:, 0:2], P, RMAX).then_inc(max_all, 1)
            token_max(0)
            ln1(0, 0)
            pool.wait_ge(w2_max, 5)
            pool.partition_all_reduce(amxB[:, 2:3], amx[:, 2:3], P, RMAX).then_inc(max2_all, 1)

            def block_steps(b, slot):
                token_max(b + 1)
                ln1(b + 1, 1 - slot)
                ln2(b)

            block_steps(0, 0)
            with nc.gpsimd.Fori(0, NB // 2 - 1) as i:
                for k in range(2):
                    block_steps(2 * i + 1 + k, 1 - k)
            ln2(NB - 1)

        @block.scalar
        def _(act):
            act.dma_start(masks_sb[:, :], masks).then_inc(dma_small, 16)
            act.dma_start(peR[:, :, :], pe_r.rearrange("p (b h) -> p b h", b=NB)).then_inc(dma_small, 16)
            for dst, src in ((g1B[:, :], g1), (be1_st, be1), (b2_st, b2), (g2B[:, :], g2), (be2B[:, :], be2)):
                act.dma_start(dst, src.unsqueeze(0).broadcast_to([P, D])).then_inc(dma_small, 16)
            with nc.allow_non_contiguous_dma(reason="small columns"):
                act.dma_start(cols[:, 0:NJ], b1.rearrange("(j p) -> p j", p=P)).then_inc(dma_small, 16)
                act.dma_start(cols[:, NJ:NJ + NC], g1.rearrange("(j p) -> p j", p=P)).then_inc(dma_small, 16)
                act.dma_start(cols[:, NJ + NC:NJ + 2 * NC], be1.rearrange("(j p) -> p j", p=P)).then_inc(dma_small, 16)
            act.dma_start(wqT_sb[:, :, :], wqT.rearrange("(c p) n -> p c n", p=P)).then_inc(dma_wqT, 16)
            act.dma_start(wfc_st, wfcT.rearrange("(c p) n -> p c n", p=P)).then_inc(dma_wfc, 16)

            banks = acc + hps + aux
            for h in range(NH):
                act.wait_ge(wr_ready, h + 1)
                act.activation(wrB[:, h], banks[h][:, :], ACT.Copy).then_inc(wrB_ready, 1)
            act.wait_ge(wfc_ready, 1)
            act.activation(wfcS[:, :], acc[0][:, :], ACT.Copy).then_inc(wfcS_ready, 1)

            def exp_scores(n, slot):
                act.wait_ge(rs_ready, n + 1)
                if not isinstance(n, int) or n >= 2:
                    act.wait_ge(xbar_done, n - 1)
                act.activation(ee[:, slot], rs[:, :, :], ACT.Exp).then_inc(e_ready, 1)

            def o1_chunk(n, slot, c):
                act.wait_ge(zT_done, NC * n + c + 1)
                act.activation(o1hi[:, slot, c], aux[c % 2][:, :], ACT.Identity,
                               bias=be1S[:, c:c + 1], scale=g1S[:, c:c + 1]).then_inc(o1hi_ready, 1)
                if c >= 2 or not isinstance(n, int) or n > 0:
                    act.wait_ge(o1lo_ready, NC * n + c - 1)
                act.activation(o1f[:, c % 2], aux[c % 2][:, :], ACT.Identity,
                               bias=be1S[:, c:c + 1], scale=g1S[:, c:c + 1]).then_inc(o1f_ready, 1)

            def hidden(g, j):
                s = j % 2
                act.wait_ge(ffn1_done, g + 1)
                if not isinstance(g, int) or g >= 2:
                    act.wait_ge(ffn2_done, g - 1)
                act.activation(hhi[:, s], hps[s][:, :], ACT.Relu,
                               bias=b1S[:, j:j + 1], scale=c1).then_inc(hhi_ready, 1)
                if not isinstance(g, int) or g >= 2:
                    act.wait_ge(hlo_ready, g - 1)
                act.activation(hf[:, s], hps[s][:, :], ACT.Relu,
                               bias=b1S[:, j:j + 1], scale=c1).then_inc(hf_ready, 1)

            exp_scores(0, 0)
            act.wait_ge(scales_ready, 1)
            for q in range(4):
                act.activation(w1hi[:, :, q * D:(q + 1) * D], w1_st[:, q], ACT.Copy,
                               scale=sc[:, 0:1]).then_inc(w1hi_ready, 1)
            for c in range(NC):
                o1_chunk(0, 0, c)
            hidden(0, 0)
            act.wait_ge(w2_scale, 1)
            act.wait_ge(w1lo_ready, 4)
            for q in range(4):
                act.wait_ge(dma_w2[q % 2], 16 * (3 + q // 2))
                act.activation(w2hi[:, 4 * q:4 * q + 4], w2_st[q % 2], ACT.Copy,
                               scale=sc[:, 3:4]).then_inc(w2hi_ready, 1)

            def block_steps(b, slot, front):
                for j in range(NJ):
                    if front or j < NJ - 1:
                        hidden(NJ * b + j + 1, (j + 1) % NJ)
                    if front and j == 6:
                        exp_scores(b + 1, 1 - slot)
                    if front and j in (13, 14):
                        for c in (0, 1) if j == 13 else (2, 3):
                            o1_chunk(b + 1, 1 - slot, c)

            block_steps(0, 0, True)
            with nc.scalar.Fori(0, NB // 2 - 1) as i:
                for k in range(2):
                    block_steps(2 * i + 1 + k, 1 - k, True)
            block_steps(NB - 1, 1, False)

        @block.vector
        def _(dve):
            def scores(n, slot, lo, hi):
                if lo == 0:
                    dve.wait_ge(dma_x[slot], 32 * (n // 2 + 1) if isinstance(n, int) else 16 * (n + (2 - slot)))
                for i in range(lo, hi):
                    t, h = i // NH, i % NH
                    if i >= 2 or not isinstance(n, int) or n > 0:
                        dve.wait_ge(r_ready, NT * NH * n + i - 1)
                    dve.scalar_tensor_tensor(scr[:, i % 2], xb[:, slot, t], 1.0, wrB[:, h], ALU.mult, ALU.mult,
                                             accum_out=rr[:, t, h:h + 1]).then_inc(r_ready, 1)

            def scores_max(n):
                dve.wait_ge(r_ready, NT * NH * (n + 1))
                dve.tensor_tensor(rp[:, :, :], rr[:, :, :], peR[:, n, :].unsqueeze(1).broadcast_to([P, NT, NH]),
                                  ALU.add).then_inc(rp_ready, 1)
                dve.wait_ge(rp_ready, n + 1)
                dve.tensor_reduce(rmx[:, :], rp[:, :, :].rearrange("p t h -> p h t"), AX.X,
                                  ALU.max).then_inc(rmx_ready, 1)

            def scores_shift(n):
                dve.wait_ge(mx_ready, n + 1)
                if not isinstance(n, int) or n > 0:
                    dve.wait_ge(e_ready, n)
                dve.tensor_tensor(rs[:, :, :], rp[:, :, :], mxB[:, :].unsqueeze(1).broadcast_to([P, NT, NH]),
                                  ALU.subtract).then_inc(rs_ready, 1)

            def exp_sum(n, slot):
                dve.wait_ge(e_ready, n + 1)
                dve.tensor_reduce(es[:, slot], ee[:, slot].rearrange("p t h -> p h t"), AX.X,
                                  ALU.add).then_inc(es_ready, 1)

            def xbar_out(n):
                dve.wait_ge(xbar_done, n + 1)
                if not isinstance(n, int) or n > 0:
                    dve.wait_ge(o_done, n)
                dve.tensor_copy(xbT[:, :, :], aux[0][:, 0:NC * NH].rearrange("p (c h) -> p c h", c=NC)).then_inc(xbar_copied, 1)
                dve.tensor_copy(zT[:, :], aux[0][0:SPB, 32:40]).then_inc(xbar_copied, 1)
                dve.reciprocal(rden[:, :], aux[0][:, 40:48]).then_inc(xbar_copied, 1)

            def head_rows(n):
                dve.wait_ge(o_done, n + 1)
                dve.wait_ge(xbar_copied, 3 * (n + 1))
                if isinstance(n, int) and n == 0:
                    dve.wait_ge(consts_set, 2)
                else:
                    dve.wait_ge(ao_done, n)
                for odd in range(2):
                    rows = slice(64 * odd, 64 * odd + 64)
                    heads = slice(odd, NH, 2)
                    src = aux[1][rows, odd:odd + 31:10].unsqueeze(2).broadcast_to([64, 4, 16])
                    dve.tensor_tensor(ocx[rows, heads, :], src,
                                      rden[rows, heads].unsqueeze(2).broadcast_to([64, 4, 16]),
                                      ALU.mult).then_inc(ocx_ready, 1)

            def add_attention(n, slot):
                dve.wait_ge(ao_done, n + 1)
                if not isinstance(n, int) or n > 0:
                    dve.wait_ge(zT_done, NC * n)
                    dve.wait_ge(o1b_ready, NT * n)
                for t in range(NT):
                    dve.tensor_tensor(yz[:, t], xb[:, slot, t], aux[0][:, :], ALU.add).then_inc(y_ready, 1)

            def stats(n, k, src, src_sem, bn_sem, mv_sem):
                for t in range(NT):
                    dve.wait_ge(src_sem, NT * n + t + 1)
                    dve.bn_stats(bn[:, k, t], src[:, t]).then_inc(bn_sem, 1)
                for t in range(NT):
                    dve.wait_ge(bn_sem, NT * n + t + 1)
                    dve.sem_inc(dve_passed, 1)
                    dve.bn_aggr(mv[:, k, t], bn[:, k, t]).then_inc(mv_sem, 1)

            def normalise(n):
                dve.wait_ge(rstd_ready, n + 1)
                for t in range(NT):
                    dve.tensor_scalar(yz[:, t], yz[:, t], mv[:, 0, t, 0:1], rstd[:, 0, t:t + 1],
                                      ALU.subtract, ALU.mult).then_inc(z_ready, 1)

            def o1_low(n, slot, c):
                dve.wait_ge(o1f_ready, NC * n + c + 1)
                dve.wait_ge(o1hi_ready, NC * n + c + 1)
                dve.tensor_tensor(o1lo[:, slot, c], o1f[:, c % 2], o1hi[:, slot, c],
                                  ALU.subtract).then_inc(o1lo_ready, 1)

            def hidden_low(g, s):
                dve.wait_ge(hf_ready, g + 1)
                dve.wait_ge(hhi_ready, g + 1)
                if not isinstance(g, int) or g >= 2:
                    dve.wait_ge(ffn2_done, g - 1)
                dve.tensor_tensor(hlo[:, s], hf[:, s], hhi[:, s], ALU.subtract).then_inc(hlo_ready, 1)

            def add_ffn(b, slot):
                dve.wait_ge(ffn2_done, NJ * (b + 1))
                dve.wait_ge(o1b_ready, NT * (b + 1))
                if not isinstance(b, int) or b > 0:
                    dve.wait_ge(dma_out, 16 * b)
                for t in range(NT):
                    dve.scalar_tensor_tensor(y2[:, t], acc[t][:, :], c2, o1b[:, slot, t],
                                             ALU.mult, ALU.add).then_inc(y2_ready, 1)

            def power_of_two(cols_, first):
                step = [first]

                def then(ins):
                    step[0] += 1
                    ins.then_inc(scale_step, 1)
                    dve.wait_ge(scale_step, step[0])

                then(dve.tensor_scalar(bnd[:, cols_], bnd[:, cols_], 1e-30, None, ALU.max))
                then(dve.tensor_scalar(pw[:, cols_].bitcast(u32), bnd[:, cols_].bitcast(u32), 0x7F800000, None,
                                       ALU.bitwise_and))
                then(dve.tensor_scalar(sc[:, cols_].bitcast(u32), pw[:, cols_].bitcast(u32), 0x7F800000, None,
                                       ALU.bitwise_xor))
                then(dve.tensor_scalar(sc[:, cols_], sc[:, cols_], 2.0 ** 12, None, ALU.mult))
                then(dve.tensor_scalar(isc[:, cols_], pw[:, cols_], 2.0 ** -13, None, ALU.mult))
                return then

            dve.wait_ge(dma_small, 16 * 10)
            dve.tensor_tensor(addB[:, :], be1_st, b2_st, ALU.add).then_inc(addB_ready, 1)
            dve.tensor_reduce(amx[:, 1:2], cols[:, 0:NJ], AX.X, ALU.max, apply_absolute_value=True).then_inc(small_max, 1)
            dve.tensor_reduce(bnd[:, 4:5], g1B[:, :], AX.X, ALU.max, apply_absolute_value=True).then_inc(small_max, 1)
            dve.tensor_reduce(bnd[:, 5:6], be1_st, AX.X, ALU.max, apply_absolute_value=True).then_inc(small_max, 1)
            dve.wait_ge(wrB_ready, NH)
            scores(0, 0, 0, NT * NH)
            scores_max(0)
            for q in range(4):
                dve.wait_ge(dma_w1[q], 16)
                dve.tensor_reduce(wmx[:, q:q + 1], w1_st[:, q], AX.XY, ALU.max,
                                  apply_absolute_value=True).then_inc(w1_max, 1)
            dve.wait_ge(w1_max, 4)
            dve.wait_ge(small_max, 3)
            dve.tensor_reduce(amx[:, 0:1], wmx[:, 0:4], AX.X, ALU.max).then_inc(w1_max, 1)
            scores_shift(0)
            exp_sum(0, 0)
            xbar_out(0)
            head_rows(0)
            dve.wait_ge(max_all, 1)
            dve.tensor_copy(bnd[:, 0:1], amxB[:, 0:1]).then_inc(bound_ready, 1)
            dve.scalar_tensor_tensor(bnd[:, 1:2], bnd[:, 4:5], 23.0, bnd[:, 5:6], ALU.mult, ALU.add).then_inc(bound_ready, 1)
            dve.wait_ge(bound_ready, 2)
            dve.scalar_tensor_tensor(bnd[:, 6:7], bnd[:, 1:2], float(D), amxB[:, 0:1], ALU.mult, ALU.mult).then_inc(bound_ready, 1)
            dve.wait_ge(bound_ready, 3)
            dve.tensor_tensor(bnd[:, 2:3], bnd[:, 6:7], amxB[:, 1:2], ALU.add).then_inc(bound_ready, 1)
            dve.wait_ge(bound_ready, 4)
            then = power_of_two(slice(0, 3), 0)
            then(dve.tensor_tensor(cc[:, 0:1], isc[:, 0:1], isc[:, 1:2], ALU.mult))
            then(dve.tensor_tensor(c1, cc[:, 0:1], sc[:, 2:3], ALU.mult))
            then(dve.tensor_scalar(b1S, cols[:, 0:NJ], sc[:, 2:3], None, ALU.mult))
            then(dve.tensor_scalar(colsS[:, NJ:], cols[:, NJ:], sc[:, 1:2], None, ALU.mult))
            dve.tensor_copy(cc[:, 3:4], sc[:, 0:1]).then_inc(scales_ready, 1)
            add_attention(0, 0)
            stats(0, 0, yz, y_ready, bn_ready, mv_ready)
            for q in range(4):
                dve.wait_ge(w1hi_ready, q + 1)
                dve.scalar_tensor_tensor(w1lo[:, :, q * D:(q + 1) * D], w1_st[:, q], sc[:, 0:1],
                                         w1hi[:, :, q * D:(q + 1) * D], ALU.mult, ALU.subtract).then_inc(w1lo_ready, 1)
                if q == 0:
                    normalise(0)
            for c in range(NC):
                o1_low(0, 0, c)
            hidden_low(0, 0)
            for q in range(4):
                dve.wait_ge(dma_w2[q % 2], 16 * (1 + q // 2))
                dve.tensor_reduce(wmx[:, 8 + q:9 + q], w2_st[q % 2], AX.XY, ALU.max,
                                  apply_absolute_value=True).then_inc(w2_max, 1)
            dve.wait_ge(w2_max, 4)
            dve.tensor_reduce(amx[:, 2:3], wmx[:, 8:12], AX.X, ALU.max).then_inc(w2_max, 1)
            dve.wait_ge(max2_all, 1)
            dve.tensor_copy(bnd[:, 3:4], amxB[:, 2:3]).then_inc(bound_ready, 1)
            dve.wait_ge(bound_ready, 5)
            then = power_of_two(slice(3, 4), 9)
            then(dve.tensor_tensor(c2, isc[:, 2:3], isc[:, 3:4], ALU.mult))
            dve.tensor_copy(cc[:, 3:4], sc[:, 3:4]).then_inc(w2_scale, 1)
            for q in range(4):
                dve.wait_ge(w2hi_ready, q + 1)
                dve.scalar_tensor_tensor(w2lo[:, 4 * q:4 * q + 4], w2_st[q % 2], sc[:, 3:4],
                                         w2hi[:, 4 * q:4 * q + 4], ALU.mult, ALU.subtract).then_inc(w2lo_ready, 1)

            R_AT = [0, 4, 11, 18, 25, 32]

            def block_steps(b, slot, front):
                n, nslot = b + 1, 1 - slot
                for j in range(NJ):
                    if front and j == 8:
                        xbar_out(n)
                    if front and j == 9:
                        head_rows(n)
                    if front or j < NJ - 1:
                        hidden_low(NJ * b + j + 1, (j + 1) % 2)
                    if not front:
                        continue
                    if j < 5:
                        scores(n, nslot, R_AT[j], R_AT[j + 1])
                    if j == 4:
                        scores_max(n)
                    if j == 5:
                        scores_shift(n)
                    if j == 6:
                        exp_sum(n, nslot)
                    if j == 10:
                        add_attention(n, nslot)
                    if j == 11:
                        stats(n, 0, yz, y_ready, bn_ready, mv_ready)
                    if j == 12:
                        normalise(n)
                    if j in (13, 14):
                        for c in (0, 1) if j == 13 else (2, 3):
                            o1_low(n, nslot, c)
                add_ffn(b, slot)
                stats(b, 1, y2, y2_ready, bn2_ready, mv2_ready)

            block_steps(0, 0, True)
            with nc.vector.Fori(0, NB // 2 - 1) as i:
                for k in range(2):
                    block_steps(2 * i + 1 + k, 1 - k, True)
            block_steps(NB - 1, 1, False)

        @block.tensor
        def _(te):
            banks = acc + hps + aux
            te.wait_ge(dma_small, 16 * 10)
            te.wait_ge(dma_wq, 16)
            for h in range(NH):
                rows = slice(64 * (h % 2), 64 * (h % 2) + 64)
                te.matmul(banks[h][:, :], ones[rows, :], wq_st[rows, h // 2, :],
                          start=True, stop=True).then_inc(wr_ready, 1)
            te.wait_ge(dma_wfc, 16)
            te.wait_ge(wrB_ready, NH)
            for c in range(NC):
                mm = te.matmul(acc[0][:, :], fold, wfc_st[:, c], start=(c == 0), stop=(c == NC - 1))
            mm.then_inc(wfc_ready, 1)

            def weighted_x(n, slot):
                te.wait_ge(es_ready, n + 1)
                if not isinstance(n, int) or n > 0:
                    te.wait_ge(o1f_ready, NC * n - 1)
                for c in range(NC):
                    for t in range(NT):
                        te.matmul(aux[0][:, c * NH:(c + 1) * NH], xb[:, slot, t, c * P:(c + 1) * P],
                                  ee[:, slot, t], start=(t == 0), stop=(t == NT - 1))
                te.matmul(aux[0][0:SPB, 32:40], ind, es[:, slot], start=True, stop=True)
                te.matmul(aux[0][:, 40:48], ones, es[:, slot], start=True, stop=True).then_inc(xbar_done, 1)

            def project_q(n, slot):
                te.wait_ge(xbar_copied, 3 * (n + 1))
                if not isinstance(n, int) or n > 0:
                    te.wait_ge(o1f_ready, NC * n)
                for m in range(NC):
                    for c in range(NC):
                        te.matmul(aux[1][:, m * NH:(m + 1) * NH], wqT_sb[:, c, m * P:(m + 1) * P], xbT[:, c],
                                  start=(c == 0), stop=False)
                    mm = te.matmul(aux[1][:, m * NH:(m + 1) * NH], peb[:, slot, m * P:(m + 1) * P], zT[:, :],
                                   start=False, stop=True)
                mm.then_inc(o_done, 1)

            def project_out(n):
                te.wait_ge(ocx_ready, 2 * (n + 1))
                te.wait_ge(xbar_copied, 3 * (n + 1))
                te.matmul(aux[0][:, :], ocx[:, :, :].rearrange("p h r -> p (h r)"), wfcS[:, :],
                          start=True, stop=True).then_inc(ao_done, 1)

            def transpose_z(n, c):
                te.wait_ge(z_ready, NT * (n + 1))
                if c >= 2:
                    te.wait_ge(o1f_ready, NC * n + c - 1)
                for t in range(NT):
                    mm = te.transpose(aux[c % 2][:, t * P:(t + 1) * P], yz[:, t, c * P:(c + 1) * P], ident)
                mm.then_inc(zT_done, 1)

            def ffn1(g, j, slot):
                s = j % 2
                if not isinstance(g, int) or g >= 2:
                    te.wait_ge(hf_ready, g - 1)
                k = 0
                for c in range(NC):
                    cols_ = slice(j * P, (j + 1) * P)
                    for w, o in ((w1hi, o1hi), (w1hi, o1lo), (w1lo, o1hi)):
                        mm = te.matmul(hps[s][:, :], w[:, c, cols_], o[:, slot, c],
                                       start=(k == 0), stop=(k == 3 * NC - 1))
                        k += 1
                mm.then_inc(ffn1_done, 1)

            def ffn2(g, j, b):
                s = j % 2
                te.wait_ge(hhi_ready, g + 1)
                for t in range(NT):
                    if j == 0 and (not isinstance(b, int) or b > 0):
                        te.wait_ge(y2_ready, NT * (b - 1) + t + 1)
                    tok = slice(t * P, (t + 1) * P)
                    te.matmul(acc[t][:, :], hhi[:, s, tok], w2hi[:, j], start=(j == 0), stop=False)
                    te.matmul(acc[t][:, :], hhi[:, s, tok], w2lo[:, j], start=False, stop=False)
                te.wait_ge(hlo_ready, g + 1)
                for t in range(NT):
                    tok = slice(t * P, (t + 1) * P)
                    mm = te.matmul(acc[t][:, :], hlo[:, s, tok], w2hi[:, j], start=False, stop=(j == NJ - 1))
                mm.then_inc(ffn2_done, 1)

            te.wait_ge(dma_x[0], 32)
            weighted_x(0, 0)
            te.wait_ge(dma_wqT, 16)
            project_q(0, 0)
            te.wait_ge(wfcS_ready, 1)
            project_out(0)
            for c in range(NC):
                transpose_z(0, c)
            te.wait_ge(w1lo_ready, 4)
            te.wait_ge(o1hi_ready, NC)
            te.wait_ge(o1lo_ready, NC)
            ffn1(0, 0, 0)
            te.wait_ge(w2lo_ready, 4)

            def block_steps(b, slot, front):
                n, nslot = b + 1, 1 - slot
                for j in range(NJ):
                    if front:
                        if j == 8:
                            weighted_x(n, nslot)
                        if j == 9:
                            project_q(n, nslot)
                        if j == 10:
                            project_out(n)
                        if j in (13, 14):
                            for c in (0, 1) if j == 13 else (2, 3):
                                transpose_z(n, c)
                        if j == NJ - 1:
                            te.wait_ge(o1hi_ready, NC * (n + 1))
                            te.wait_ge(o1lo_ready, NC * (n + 1))
                            ffn1(NJ * n, 0, nslot)
                    if j < NJ - 1:
                        ffn1(NJ * b + j + 1, j + 1, slot)
                    ffn2(NJ * b + j, j, b)

            block_steps(0, 0, True)
            with nc.tensor.Fori(0, NB // 2 - 1) as i:
                for k in range(2):
                    block_steps(2 * i + 1 + k, 1 - k, True)
            block_steps(NB - 1, 1, False)


def kernel(x, L0_conv_Wq, L0_conv_Wfc, L0_conv_W1, L0_conv_b1, L0_conv_W2, L0_conv_b2,
           L0_conv_g1, L0_conv_be1, L0_conv_g2, L0_conv_be2):
    import numpy as np
    import concourse.bacc as bacc
    from concourse.bass_utils import run_bass_kernel_spmd

    S = x.shape[0]
    pos = np.arange(S, dtype=np.float32)[:, None]
    div = np.exp(np.arange(0, D, 2, dtype=np.float32) * np.float32(-np.log(10000.0) / D)).astype(np.float32)
    ang = (pos * div).astype(np.float32)
    pe = np.zeros((S, D), np.float32)
    pe[:, 0::2] = np.sin(ang)
    pe[:, 1::2] = np.cos(ang)
    pr = pe.reshape(NB, SPB, NH, DEPTH).sum(-1, dtype=np.float64).astype(np.float32)
    p = np.arange(P)
    pe_r = np.ascontiguousarray(pr[:, p // 4, :].transpose(1, 0, 2).reshape(P, NB * NH))
    masks = np.concatenate([np.eye(P), (p[:, None] % 64 == p[None, :] % 64), np.ones((P, P)),
                            (p[:, None] // 4 == np.arange(SPB)[None, :])], axis=1).astype(np.float32)
    arrays = {
        "x": np.ascontiguousarray(x).reshape(-1, D),
        "wq": np.ascontiguousarray(L0_conv_Wq),
        "wqT": np.ascontiguousarray(np.asarray(L0_conv_Wq).T),
        "wfcT": np.ascontiguousarray(np.asarray(L0_conv_Wfc).T),
        "w1T": np.ascontiguousarray(np.asarray(L0_conv_W1).T),
        "b1": np.ascontiguousarray(L0_conv_b1),
        "w2T": np.ascontiguousarray(np.asarray(L0_conv_W2).T),
        "b2": np.ascontiguousarray(L0_conv_b2),
        "g1": np.ascontiguousarray(L0_conv_g1),
        "be1": np.ascontiguousarray(L0_conv_be1),
        "g2": np.ascontiguousarray(L0_conv_g2),
        "be2": np.ascontiguousarray(L0_conv_be2),
        "pe": pe,
        "pe_r": pe_r,
        "masks": masks,
    }
    nc = bacc.Bacc("TRN2", target_bir_lowering=False, num_devices=1)
    args = [nc.dram_tensor(f"in_{k}", a.shape, mybir.dt.float32, kind="ExternalInput").ap() for k, a in arrays.items()]
    out = nc.dram_tensor("out_y", (NB * TB, D), mybir.dt.float32, kind="ExternalOutput").ap()
    conv_seq_kernel(nc, *args, out)
    r = run_bass_kernel_spmd(nc, [{f"in_{k}": a for k, a in arrays.items()}], core_ids=[0])
    return r.results[0]["out_y"].reshape(x.shape)
```

```python
import concourse.bass as bass
from concourse import mybir
from contextlib import ExitStack

D = 512
DFF = 2048
NH = 8
DEPTH = D // NH
TB = 512
NB = 16
P = 128
NT = TB // P
NC = D // P
NP = 3
NJ = DFF // P
SPB = TB // 16
EPS = 1e-5
Z_AT = {12: (0, 1), 13: (2, 3)}


def conv_seq_kernel(nc, x, wq, wqT, wfcT, w1T, b1, w2T, b2, g1, be1, g2, be2, pe_parts, pe_r, masks, out):
    f32 = mybir.dt.float32
    f16 = mybir.dt.float16
    bf16 = mybir.dt.bfloat16
    u32 = mybir.dt.uint32
    ALU = mybir.AluOpType
    ACT = mybir.ActivationFunctionType
    AX = mybir.AxisListType

    x_v = x.rearrange("(b p t) f -> b p (t f)", p=P, t=NT)
    out_v = out.rearrange("(b p t) f -> b p (t f)", p=P, t=NT)
    pe_v = pe_parts.rearrange("(b s) g f -> b s g f", s=SPB).bitcast(bf16)
    w1_v = w1T.rearrange("(c p) (q n) -> q p c n", p=P, q=4)
    w2_v = w2T.rearrange("(q j p) n -> q p j n", p=P, q=4)

    ctx = ExitStack()
    with ctx:
        def sb(name, shape, dt=f32):
            return ctx.enter_context(nc.sbuf_tensor(name, shape, dt))

        def pb(name):
            return ctx.enter_context(nc.psum_tensor(name, [P, 512], f32))

        def sem(name):
            return ctx.enter_context(nc.semaphore(name))

        w1hi = sb("w1hi", [P, NC, DFF], f16)
        w1lo = sb("w1lo", [P, NC, DFF], f16)
        w2 = sb("w2", [P, 2, NJ, D], f16)
        w2hi, w2lo = w2[:, 0], w2[:, 1]
        wqp = sb("wqp", [P, NP, NC, D], bf16)
        wrB = sb("wrB", [P, NH, D])
        wfcS = sb("wfcS", [P, D])
        g1B = sb("g1B", [P, D])
        addB = sb("addB", [P, D])
        g2B = sb("g2B", [P, D])
        be2B = sb("be2B", [P, D])
        masks_sb = sb("masks_sb", [P, 4 * P])
        ident = masks_sb[:, 0:P]
        fold = masks_sb[:, P:2 * P]
        ones = masks_sb[:, 2 * P:3 * P]
        masks_b = sb("masks_b", [P, 2, P], bf16)
        peR = sb("peR", [P, NB, NH])
        cols = sb("cols", [P, NJ + 2 * NC])
        colsS = sb("colsS", [P, NJ + 2 * NC])
        b1S = colsS[:, 0:NJ]
        g1S = colsS[:, NJ:NJ + NC]
        be1S = colsS[:, NJ + NC:NJ + 2 * NC]
        xb = sb("xb", [P, 2, NT, D])
        peb = sb("peb", [SPB, 2, NP, D], bf16)
        xp = sb("xp", [P, NP, NT, D], bf16)
        yz = sb("yz", [P, NT, D])
        o1b = sb("o1b", [P, 2, NT, D])
        y2 = sb("y2", [P, NT, D])
        o1f = sb("o1f", [P, 2, TB])
        o1hi = sb("o1hi", [P, 2, NC, TB], f16)
        o1lo = sb("o1lo", [P, 2, NC, TB], f16)
        hf = sb("hf", [P, 2, TB])
        hhi = sb("hhi", [P, 2, TB], f16)
        hlo = sb("hlo", [P, 2, TB], f16)
        scr = sb("scr", [P, 2, D])
        rr = sb("rr", [P, NT, NH])
        rp = sb("rp", [P, NT, NH])
        rs = sb("rs", [P, NT, NH])
        ee = sb("ee", [P, NT, NH])
        ep = sb("ep", [P, NT, NP, NH], bf16)
        rmx = sb("rmx", [P, NH])
        mxB = sb("mxB", [P, NH])
        xs = sb("xs", [P, NC + 2, NH])
        xsp = sb("xsp", [P, NC + 2, NP, NH], bf16)
        osum = sb("osum", [P, NC])
        rden = sb("rden", [P, NH])
        ocx = sb("ocx", [P, NH, 16])
        bn = sb("bn", [P, 2, NT, 6])
        mv = sb("mv", [P, 2, NT, 2])
        var_eps = sb("var_eps", [P, 2, NT])
        rstd = sb("rstd", [P, 2, NT])
        half = sb("half", [P, 2, NT])
        wr_c = sb("wr_c", [P, NC, NH])
        sqp = sb("sqp", [P, 9])
        sq = sb("sq", [P, 4])
        norm2 = sb("norm2", [P, 4])
        norm = sb("norm", [P, 4])
        gmax = sb("gmax", [P, 1])
        bnd = sb("bnd", [P, 6])
        pw = sb("pw", [P, 4])
        sc = sb("sc", [P, 4])
        isc = sb("isc", [P, 4])
        cc = sb("cc", [P, 4])
        c1 = cc[:, 1:2]
        c2 = cc[:, 2:3]

        w1_st = w2[:, :, :, :].rearrange("p a j n -> p (a j n)").bitcast(f32).rearrange(
            "p (q c n) -> p q c n", q=4, c=NC)
        wq_st = y2
        wqT_st = o1b[:, 0]
        wfc_st = o1b[:, 1]
        xT_st = w1hi[:, :, :].rearrange("p c n -> p (c n)").bitcast(f32)[:, 0:NC * TB].rearrange(
            "p (c n) -> p c n", c=NC)
        w2_st = [y2[:, :, :], o1b[:, 1]]
        be1_st = o1f[:, 0, :]
        b2_st = o1f[:, 1, :]

        acc = [pb(f"acc{t}") for t in range(NT)]
        hps = [pb(f"hps{t}") for t in range(2)]
        aux = [pb(f"aux{t}") for t in range(2)]

        dma_x = [sem("dma_x0"), sem("dma_x1")]
        dma_small, dma_wq, dma_wqT, dma_wfc = sem("dma_small"), sem("dma_wq"), sem("dma_wqT"), sem("dma_wfc")
        dma_w1 = [sem(f"dma_w1_{q}") for q in range(4)]
        dma_w2 = [sem(f"dma_w2_{q}") for q in range(2)]
        dma_out = sem("dma_out")
        wr_ready, wrB_ready, wfc_ready, wfcS_ready = sem("wr_ready"), sem("wrB_ready"), sem("wfc_ready"), sem("wfcS_ready")
        consts_set, masks_ready = sem("consts_set"), sem("masks_ready")
        xT_done, xT_ready, wrc_ready, r0_done = sem("xT_done"), sem("xT_ready"), sem("wrc_ready"), sem("r0_done")
        wq_split = sem("wq_split")
        w1_squares, w2_squares, squares_ready, small_ready = sem("w1_squares"), sem("w2_squares"), sem("squares_ready"), sem("small_ready")
        norm2_ready, norm_ready, norm2_w2, norm_w2 = sem("norm2_ready"), sem("norm_ready"), sem("norm2_w2"), sem("norm_w2")
        bound_ready, scale_step, scales_ready = sem("bound_ready"), sem("scale_step"), sem("scales_ready")
        w2_scale = sem("w2_scale")
        w1hi_ready, w1lo_ready, w2hi_ready, w2lo_ready = sem("w1hi_ready"), sem("w1lo_ready"), sem("w2hi_ready"), sem("w2lo_ready")
        x1_ready, d1_ready, x2_ready, x3_ready = sem("x1_ready"), sem("d1_ready"), sem("x2_ready"), sem("x3_ready")
        addB_ready = sem("addB_ready")
        ffn1_done, ffn2_done = sem("ffn1_done"), sem("ffn2_done")
        hhi_ready, hf_ready, hlo_ready = sem("hhi_ready"), sem("hf_ready"), sem("hlo_ready")
        r_ready, rp_ready, rmx_ready, mx_ready, rs_ready = sem("r_ready"), sem("rp_ready"), sem("rmx_ready"), sem("mx_ready"), sem("rs_ready")
        e_ready, e1_ready, e_split = sem("e_ready"), sem("e1_ready"), sem("e_split")
        xbar_done, xs_ready, xs_split, rden_ready = sem("xbar_done"), sem("xs_ready"), sem("xs_split"), sem("rden_ready")
        osum_ready = sem("osum_ready")
        o_done, ocx_ready, ao_done = sem("o_done"), sem("ocx_ready"), sem("ao_done")
        y_ready, bn_ready, mv_ready, z_ready, zT_done = sem("y_ready"), sem("bn_ready"), sem("mv_ready"), sem("z_ready"), sem("zT_done")
        var_ready, rstd_ready = [sem("var1_ready"), sem("var2_ready")], [sem("rstd1_ready"), sem("rstd2_ready")]
        o1hi_ready, o1f_ready, o1lo_ready = sem("o1hi_ready"), sem("o1f_ready"), sem("o1lo_ready")
        o1g_ready, o1b_ready = sem("o1g_ready"), sem("o1b_ready")
        y2_ready, bn2_ready, mv2_ready = sem("y2_ready"), sem("bn2_ready"), sem("mv2_ready")
        z2g_ready, out_ready = sem("z2g_ready"), sem("out_ready")

        dve_passed, pool_passed = sem("dve_passed"), sem("pool_passed")

        block = ctx.enter_context(nc.Block())

        def x_loaded(n, slot):
            return 16 * (n - slot) + 32

        @block.sync
        def _(sp):
            def load_x(b, slot):
                sp.dma_start(xb[:, slot].rearrange("p t f -> p (t f)"), x_v[b]).then_inc(dma_x[slot], 16)
                sp.dma_start(peb[:, slot], pe_v[b]).then_inc(dma_x[slot], 16)

            sp.dma_start(wqT_st, wqT.rearrange("(c p) n -> p c n", p=P)).then_inc(dma_wqT, 16)
            load_x(0, 0)
            for q in range(4):
                sp.dma_start(w1_st[:, q], w1_v[q]).then_inc(dma_w1[q], 16)
            sp.dma_start(wq_st[:, :, :], wq.rearrange("(c p) n -> p c n", p=P)).then_inc(dma_wq, 16)
            sp.dma_start(wfc_st, wfcT.rearrange("(c p) n -> p c n", p=P)).then_inc(dma_wfc, 16)
            load_x(1, 1)
            for n in range(8):
                if n == 0:
                    sp.wait_ge(wr_ready, NH)
                if n == 1:
                    sp.wait_ge(wfc_ready, 1)
                if 2 <= n < 6:
                    sp.wait_ge(w2_squares, n - 1)
                if n >= 6:
                    sp.wait_ge(w2hi_ready, n - 5)
                    sp.wait_ge(w2lo_ready, n - 5)
                sp.dma_start(w2_st[n % 2], w2_v[n % 4]).then_inc(dma_w2[n % 2], 16)

            def next_x(n, slot):
                sp.wait_ge(y_ready, NT * (n - 1))
                load_x(n, slot)

            def store(b):
                sp.wait_ge(out_ready, NT * (b + 1))
                sp.dma_start(out_v[b], y2[:, :, :].rearrange("p t f -> p (t f)")).then_inc(dma_out, 16)

            next_x(2, 0)
            next_x(3, 1)
            with nc.sync.Fori(0, NB // 2 - 2) as i:
                for par in range(2):
                    store(2 * i + par)
                    next_x(2 * i + par + 4, par)
            for b in range(NB - 4, NB - 1):
                store(b)
            for t in range(NT):
                sp.wait_ge(out_ready, NT * (NB - 1) + t + 1)
                sp.dma_start(out_v[NB - 1][:, t * D:(t + 1) * D], y2[:, t]).then_inc(dma_out, 16)
            sp.wait_ge(dma_out, 16 * (NB - 1 + NT))

        @block.gpsimd
        def _(pool):
            RMAX = bass.bass_isa.ReduceOp.max
            RADD = bass.bass_isa.ReduceOp.add
            pool.memset(half[:, 0], -0.5).then_inc(consts_set, 1)
            pool.memset(half[:, 1], 0.5).then_inc(consts_set, 1)
            pool.memset(ocx[:, :, :], 0.0).then_inc(consts_set, 1)

            def passed():
                pool.sem_inc(pool_passed, 1)

            def token_max(n):
                if not isinstance(n, int) or n > 0:
                    pool.wait_ge(rs_ready, n)
                pool.wait_ge(rmx_ready, n + 1)
                passed()
                pool.partition_all_reduce(mxB[:, :], rmx[:, :], P, RMAX).then_inc(mx_ready, 1)

            def inv_std(k, mv_sem, n):
                pool.wait_ge(mv_sem, NT * (n + 1))
                passed()
                pool.tensor_scalar(var_eps[:, k], mv[:, k, :, 1], EPS, None, ALU.add).then_inc(var_ready[k], 1)
                pool.wait_ge(var_ready[k], n + 1)
                pool.tensor_tensor(rstd[:, k], var_eps[:, k], half[:, 0], ALU.pow).then_inc(rstd_ready[k], 1)

            pool.wait_ge(consts_set, 3)
            token_max(0)
            pool.wait_ge(squares_ready, 1)
            pool.partition_all_reduce(norm2[:, 0:2], sq[:, 0:2], P, RADD).then_inc(norm2_ready, 1)
            pool.wait_ge(norm2_ready, 1)
            pool.wait_ge(small_ready, 2)
            pool.tensor_tensor(norm[:, 0:3], norm2[:, 0:3], half[:, 1, 0:3], ALU.pow).then_inc(norm_ready, 1)
            inv_std(0, mv_ready, 0)
            pool.wait_ge(squares_ready, 2)
            pool.partition_all_reduce(norm2[:, 3:4], sq[:, 2:3], P, RADD).then_inc(norm2_w2, 1)
            pool.wait_ge(norm2_w2, 1)
            pool.tensor_tensor(norm[:, 3:4], norm2[:, 3:4], half[:, 1, 0:1], ALU.pow).then_inc(norm_w2, 1)
            token_max(1)
            inv_std(0, mv_ready, 1)

            with nc.gpsimd.Fori(0, NB // 2 - 1) as i:
                for k in range(2):
                    b = 2 * i + 1 + k
                    token_max(b + 1)
                    inv_std(1, mv2_ready, b - 1)
                    inv_std(0, mv_ready, b + 1)
            inv_std(1, mv2_ready, NB - 2)
            inv_std(1, mv2_ready, NB - 1)

        @block.scalar
        def _(act):
            act.dma_start(masks_sb[:, :], masks).then_inc(dma_small, 16)
            act.dma_start(peR[:, :, :], pe_r.rearrange("p (b h) -> p b h", b=NB)).then_inc(dma_small, 16)
            for dst, src in ((g1B[:, :], g1), (be1_st, be1), (b2_st, b2), (g2B[:, :], g2), (be2B[:, :], be2)):
                act.dma_start(dst, src.unsqueeze(0).broadcast_to([P, D])).then_inc(dma_small, 16)
            with nc.allow_non_contiguous_dma(reason="small columns"):
                act.dma_start(cols[:, 0:NJ], b1.rearrange("(j p) -> p j", p=P)).then_inc(dma_small, 16)
                act.dma_start(cols[:, NJ:NJ + NC], g1.rearrange("(j p) -> p j", p=P)).then_inc(dma_small, 16)
                act.dma_start(cols[:, NJ + NC:NJ + 2 * NC], be1.rearrange("(j p) -> p j", p=P)).then_inc(dma_small, 16)
            wr_banks = (hps + acc) * 2

            def exp_scores(n):
                act.wait_ge(rs_ready, n + 1)
                if not isinstance(n, int) or n > 0:
                    act.wait_ge(xbar_done, n)
                    act.wait_ge(e_split, 3 * n)
                act.activation(ee[:, :, :], rs[:, :, :], ACT.Exp).then_inc(e_ready, 1)
                act.activation(ep[:, :, 0], rs[:, :, :], ACT.Exp).then_inc(e1_ready, 1)

            def x_part1(n, slot):
                if not isinstance(n, int) or n > 0:
                    act.wait_ge(xbar_done, n)
                act.wait_ge(dma_x[slot], x_loaded(n, slot))
                act.activation(xp[:, 0], xb[:, slot], ACT.Copy).then_inc(x1_ready, 1)

            def x_part2(n):
                act.wait_ge(d1_ready, n + 1)
                act.activation(xp[:, 1], yz[:, :, :], ACT.Copy).then_inc(x2_ready, 1)

            def o1_chunk(n, slot, c):
                act.wait_ge(zT_done, NC * n + c + 1)
                act.activation(o1hi[:, slot, c], aux[c % 2][:, :], ACT.Identity,
                               bias=be1S[:, c:c + 1], scale=g1S[:, c:c + 1]).then_inc(o1hi_ready, 1)
                if c >= 2 or not isinstance(n, int) or n > 0:
                    act.wait_ge(o1lo_ready, NC * n + c - 1)
                act.activation(o1f[:, c % 2], aux[c % 2][:, :], ACT.Identity,
                               bias=be1S[:, c:c + 1], scale=g1S[:, c:c + 1]).then_inc(o1f_ready, 1)

            def hidden(g, j):
                s = j % 2
                act.wait_ge(ffn1_done, g + 1)
                if not isinstance(g, int) or g >= 2:
                    act.wait_ge(ffn2_done, g - 1)
                act.activation(hhi[:, s], hps[s][:, :], ACT.Relu,
                               bias=b1S[:, j:j + 1], scale=c1).then_inc(hhi_ready, 1)
                if not isinstance(g, int) or g >= 2:
                    act.wait_ge(hlo_ready, g - 1)
                act.activation(hf[:, s], hps[s][:, :], ACT.Relu,
                               bias=b1S[:, j:j + 1], scale=c1).then_inc(hf_ready, 1)

            for c in range(NC):
                act.wait_ge(xT_done, c + 1)
                act.activation(xT_st[:, c], acc[c][:, :], ACT.Copy).then_inc(xT_ready, 1)
            x_part1(0, 0)
            act.wait_ge(dma_small, 16 * 10)
            act.activation(colsS[:, 0:NJ], cols[:, 0:NJ], ACT.Square, accum_out=sqp[:, 8:9]).then_inc(w1_squares, 1)
            squares = hf[:, :, :].rearrange("p a n -> p (a n)").bitcast(f16).rearrange("p (c n) -> p c n", c=NC)

            def sum_squares(src, k, done):
                if k > 0:
                    act.wait_ge(w1_squares, min(k, 4) + 1)
                if k > 4:
                    act.wait_ge(w2_squares, k - 4)
                act.activation(squares, src, ACT.Square, accum_out=sqp[:, k:k + 1]).then_inc(done, 1)

            for q in range(4):
                act.wait_ge(dma_w1[q], 16)
                sum_squares(w1_st[:, q], q, w1_squares)
                if q == 1:
                    x_part2(0)
                    exp_scores(0)
            for h in range(NH):
                act.wait_ge(wr_ready, h + 1)
                act.activation(wrB[:, h], wr_banks[h][:, :], ACT.Copy).then_inc(wrB_ready, 1)
            act.wait_ge(wfc_ready, 1)
            act.activation(wfcS[:, :], acc[3][:, :], ACT.Copy).then_inc(wfcS_ready, 1)
            for q in range(2):
                act.wait_ge(dma_w2[q % 2], 16 * (1 + q // 2))
                sum_squares(w2_st[q % 2], 4 + q, w2_squares)
            act.wait_ge(scales_ready, 1)
            for c in range(NC):
                o1_chunk(0, 0, c)
            for q in range(2, 4):
                act.wait_ge(dma_w2[q % 2], 16 * (1 + q // 2))
                sum_squares(w2_st[q % 2], 4 + q, w2_squares)
            act.wait_ge(w2_squares, 4)
            hidden(0, 0)
            act.wait_ge(w2_scale, 1)
            act.wait_ge(w1lo_ready, 4)
            for q in range(4):
                act.wait_ge(dma_w2[q % 2], 16 * (3 + q // 2))
                act.activation(w2hi[:, 4 * q:4 * q + 4], w2_st[q % 2], ACT.Copy,
                               scale=sc[:, 3:4]).then_inc(w2hi_ready, 1)

            def block_steps(b, slot, front):
                for j in range(NJ):
                    if front or j < NJ - 1:
                        hidden(NJ * b + j + 1, (j + 1) % NJ)
                    if not front:
                        continue
                    if j == 0:
                        x_part1(b + 1, 1 - slot)
                    if j == 3:
                        x_part2(b + 1)
                    if j == 5:
                        exp_scores(b + 1)
                    if j in Z_AT:
                        for c in Z_AT[j]:
                            o1_chunk(b + 1, 1 - slot, c)

            block_steps(0, 0, True)
            with nc.scalar.Fori(0, NB // 2 - 1) as i:
                for k in range(2):
                    block_steps(2 * i + 1 + k, 1 - k, True)
            block_steps(NB - 1, 1, False)

        @block.vector
        def _(dve):
            def scores(n, slot, lo, hi):
                if lo == 0:
                    dve.wait_ge(dma_x[slot], x_loaded(n, slot))
                for i in range(lo, hi):
                    t, h = i // NH, i % NH
                    if i >= 2 or not isinstance(n, int) or n > 1:
                        dve.wait_ge(r_ready, NT * NH * (n - 1) + i - 1)
                    dve.scalar_tensor_tensor(scr[:, i % 2], xb[:, slot, t], 1.0, wrB[:, h], ALU.mult, ALU.mult,
                                             accum_out=rr[:, t, h:h + 1]).then_inc(r_ready, 1)

            def scores_max(n, r):
                if r is None:
                    dve.wait_ge(r_ready, NT * NH * n)
                    r = rr[:, :, :]
                dve.tensor_tensor(rp[:, :, :], r, peR[:, n, :].unsqueeze(1).broadcast_to([P, NT, NH]),
                                  ALU.add).then_inc(rp_ready, 1)
                dve.wait_ge(rp_ready, n + 1)
                dve.tensor_reduce(rmx[:, :], rp[:, :, :].rearrange("p t h -> p h t"), AX.X,
                                  ALU.max).then_inc(rmx_ready, 1)

            def scores_shift(n):
                dve.wait_ge(mx_ready, n + 1)
                if not isinstance(n, int) or n > 0:
                    dve.wait_ge(e_ready, n)
                dve.tensor_tensor(rs[:, :, :], rp[:, :, :], mxB[:, :].unsqueeze(1).broadcast_to([P, NT, NH]),
                                  ALU.subtract).then_inc(rs_ready, 1)

            def x_rest(n, slot):
                dve.wait_ge(x1_ready, n + 1)
                if not isinstance(n, int) or n > 0:
                    dve.wait_ge(zT_done, NC * n)
                    dve.wait_ge(o1b_ready, NT * n)
                dve.tensor_tensor(yz[:, :, :], xb[:, slot], xp[:, 0], ALU.subtract).then_inc(d1_ready, 1)

            def x_part3(n):
                if not isinstance(n, int) or n > 0:
                    dve.wait_ge(xbar_done, n)
                dve.wait_ge(x2_ready, n + 1)
                dve.wait_ge(d1_ready, n + 1)
                dve.tensor_tensor(xp[:, 2], yz[:, :, :], xp[:, 1], ALU.subtract).then_inc(x3_ready, 1)

            def e_parts(n):
                dve.wait_ge(e_ready, n + 1)
                dve.wait_ge(e1_ready, n + 1)
                dve.tensor_tensor(ee[:, :, :], ee[:, :, :], ep[:, :, 0], ALU.subtract).then_inc(e_split, 1)
                dve.wait_ge(e_split, 3 * n + 1)
                dve.tensor_copy(ep[:, :, 1], ee[:, :, :]).then_inc(e_split, 1)
                dve.wait_ge(e_split, 3 * n + 2)
                dve.tensor_tensor(ep[:, :, 2], ee[:, :, :], ep[:, :, 1], ALU.subtract).then_inc(e_split, 1)

            def xbar_out(n):
                dve.wait_ge(xbar_done, n + 1)
                if not isinstance(n, int) or n > 0:
                    dve.wait_ge(o_done, n)
                dve.tensor_reduce(xs[:, :, :], aux[0][:, 0:(NC + 2) * NP * NH].rearrange(
                    "p (k g h) -> p k h g", k=NC + 2, g=NP), AX.X, ALU.add).then_inc(xs_ready, 1)
                dve.wait_ge(xs_ready, n + 1)
                dve.tensor_copy(xsp[:, :, 0], xs[:, :, :]).then_inc(xs_split, 1)
                dve.reciprocal(rden[:, :], xs[:, NC]).then_inc(rden_ready, 1)
                dve.wait_ge(xs_split, 5 * n + 1)
                dve.wait_ge(rden_ready, n + 1)
                dve.tensor_tensor(xs[:, :, :], xs[:, :, :], xsp[:, :, 0], ALU.subtract).then_inc(xs_split, 1)
                dve.wait_ge(xs_split, 5 * n + 2)
                dve.tensor_copy(xsp[:, :, 1], xs[:, :, :]).then_inc(xs_split, 1)
                dve.wait_ge(xs_split, 5 * n + 3)
                dve.tensor_tensor(xsp[:, :, 2], xs[:, :, :], xsp[:, :, 1], ALU.subtract).then_inc(xs_split, 2)

            def head_rows(n):
                dve.wait_ge(o_done, n + 1)
                for odd in range(2):
                    rows = slice(64 * odd, 64 * odd + 64)
                    src = aux[1][rows, 0:NC * 26].rearrange("p (m k) -> p m k", k=26)[:, :, odd:odd + 17:8]
                    dve.tensor_reduce(osum[rows, :], src, AX.X, ALU.add).then_inc(osum_ready, 1)
                if isinstance(n, int) and n == 0:
                    dve.wait_ge(consts_set, 3)
                else:
                    dve.wait_ge(ao_done, n)
                for odd in range(2):
                    rows = slice(64 * odd, 64 * odd + 64)
                    heads = slice(odd, NH, 2)
                    dve.wait_ge(osum_ready, 2 * n + odd + 1)
                    dve.tensor_tensor(ocx[rows, heads, :], osum[rows, :].unsqueeze(2).broadcast_to([64, NC, 16]),
                                      rden[rows, heads].unsqueeze(2).broadcast_to([64, NC, 16]),
                                      ALU.mult).then_inc(ocx_ready, 1)

            def add_attention(n, slot):
                dve.wait_ge(ao_done, n + 1)
                dve.wait_ge(x2_ready, n + 1)
                dve.wait_ge(x3_ready, n + 1)
                for t in range(NT):
                    dve.tensor_tensor(yz[:, t], xb[:, slot, t], aux[0][:, :], ALU.add).then_inc(y_ready, 1)

            def stats(n, k, src, src_sem, bn_sem, mv_sem):
                for t in range(NT):
                    dve.wait_ge(src_sem, NT * n + t + 1)
                    dve.bn_stats(bn[:, k, t], src[:, t]).then_inc(bn_sem, 1)
                for t in range(NT):
                    dve.wait_ge(bn_sem, NT * n + t + 1)
                    dve.sem_inc(dve_passed, 1)
                    dve.bn_aggr(mv[:, k, t], bn[:, k, t]).then_inc(mv_sem, 1)

            def normalise(n):
                dve.wait_ge(rstd_ready[0], n + 1)
                for t in range(NT):
                    dve.tensor_scalar(yz[:, t], yz[:, t], mv[:, 0, t, 0:1], rstd[:, 0, t:t + 1],
                                      ALU.subtract, ALU.mult).then_inc(z_ready, 1)

            def o1_low(n, slot, c):
                dve.wait_ge(o1f_ready, NC * n + c + 1)
                dve.wait_ge(o1hi_ready, NC * n + c + 1)
                dve.tensor_tensor(o1lo[:, slot, c], o1f[:, c % 2], o1hi[:, slot, c],
                                  ALU.subtract).then_inc(o1lo_ready, 1)

            def hidden_low(g, s):
                dve.wait_ge(hf_ready, g + 1)
                dve.wait_ge(hhi_ready, g + 1)
                if not isinstance(g, int) or g >= 2:
                    dve.wait_ge(ffn2_done, g - 1)
                dve.tensor_tensor(hlo[:, s], hf[:, s], hhi[:, s], ALU.subtract).then_inc(hlo_ready, 1)

            def residual(n, slot, ts):
                for t in ts:
                    dve.wait_ge(z_ready, NT * n + t + 1)
                    dve.tensor_tensor(o1b[:, slot, t], yz[:, t], g1B[:, :], ALU.mult).then_inc(o1g_ready, 1)
                for t in ts:
                    dve.wait_ge(o1g_ready, NT * n + t + 1)
                    dve.tensor_tensor(o1b[:, slot, t], o1b[:, slot, t], addB[:, :], ALU.add).then_inc(o1b_ready, 1)

            def ln2(b, ts):
                dve.wait_ge(rstd_ready[1], b + 1)
                for t in ts:
                    dve.scalar_tensor_tensor(y2[:, t], y2[:, t], mv[:, 1, t, 0:1], g2B[:, :],
                                             ALU.subtract, ALU.mult).then_inc(z2g_ready, 1)
                for t in ts:
                    dve.wait_ge(z2g_ready, NT * b + t + 1)
                    dve.scalar_tensor_tensor(y2[:, t], y2[:, t], rstd[:, 1, t:t + 1], be2B[:, :],
                                             ALU.mult, ALU.add).then_inc(out_ready, 1)

            def add_ffn(b, slot):
                dve.wait_ge(ffn2_done, NJ * (b + 1))
                dve.wait_ge(o1b_ready, NT * (b + 1))
                if not isinstance(b, int) or b > 0:
                    dve.wait_ge(dma_out, 16 * b)
                for t in range(NT):
                    dve.scalar_tensor_tensor(y2[:, t], acc[t][:, :], c2, o1b[:, slot, t],
                                             ALU.mult, ALU.add).then_inc(y2_ready, 1)

            def power_of_two(cols_, first):
                step = [first]

                def then(ins):
                    step[0] += 1
                    ins.then_inc(scale_step, 1)
                    dve.wait_ge(scale_step, step[0])

                then(dve.tensor_scalar(bnd[:, cols_], bnd[:, cols_], 1e-30, None, ALU.max))
                then(dve.tensor_scalar(pw[:, cols_].bitcast(u32), bnd[:, cols_].bitcast(u32), 0x7F800000, None,
                                       ALU.bitwise_and))
                then(dve.tensor_scalar(sc[:, cols_].bitcast(u32), pw[:, cols_].bitcast(u32), 0x7F800000, None,
                                       ALU.bitwise_xor))
                then(dve.tensor_scalar(sc[:, cols_], sc[:, cols_], 2.0 ** 12, None, ALU.mult))
                then(dve.tensor_scalar(isc[:, cols_], pw[:, cols_], 2.0 ** -13, None, ALU.mult))
                return then

            def split_w1(q):
                cols_ = slice(q * D, (q + 1) * D)
                if q == 0:
                    dve.wait_ge(r0_done, 1)
                dve.tensor_scalar(w1hi[:, :, cols_], w1_st[:, q], sc[:, 0:1], None, ALU.mult).then_inc(w1hi_ready, 1)
                dve.wait_ge(w1hi_ready, q + 1)
                dve.scalar_tensor_tensor(w1lo[:, :, cols_], w1_st[:, q], sc[:, 0:1], w1hi[:, :, cols_],
                                         ALU.mult, ALU.subtract).then_inc(w1lo_ready, 1)

            dve.wait_ge(dma_wqT, 16)
            dve.tensor_reduce(wr_c[:, :, :], wqT_st.rearrange("p c (h k) -> p c h k", h=NH), AX.X,
                              ALU.add).then_inc(wrc_ready, 1)
            dve.tensor_copy(wqp[:, 0], wqT_st).then_inc(wq_split, 1)
            dve.wait_ge(wq_split, 1)
            dve.tensor_tensor(wqT_st, wqT_st, wqp[:, 0], ALU.subtract).then_inc(wq_split, 1)
            dve.wait_ge(wq_split, 2)
            dve.tensor_copy(wqp[:, 1], wqT_st).then_inc(wq_split, 1)
            dve.wait_ge(wq_split, 3)
            dve.tensor_tensor(wqp[:, 2], wqT_st, wqp[:, 1], ALU.subtract).then_inc(wq_split, 1)
            x_rest(0, 0)
            dve.wait_ge(dma_small, 16 * 10)
            dve.tensor_copy(masks_b[:, :, :], masks_sb[:, 2 * P:4 * P].rearrange("p (a n) -> p a n", a=2)).then_inc(masks_ready, 1)
            dve.wait_ge(r0_done, 1)
            scores_max(0, aux[1][:, 0:NT * NH].rearrange("p (t h) -> p t h", t=NT))
            dve.tensor_tensor(addB[:, :], be1_st, b2_st, ALU.add).then_inc(addB_ready, 1)
            dve.tensor_reduce(gmax[:, :], g1B[:, :], AX.X, ALU.max, apply_absolute_value=True).then_inc(small_ready, 1)
            dve.scalar_tensor_tensor(scr[:, 0], be1_st, 1.0, be1_st, ALU.mult, ALU.mult,
                                     accum_out=norm2[:, 2:3]).then_inc(small_ready, 1)
            scores_shift(0)
            x_part3(0)
            e_parts(0)
            xbar_out(0)
            dve.wait_ge(w1_squares, 5)
            dve.tensor_reduce(sq[:, 0:1], sqp[:, 0:4], AX.X, ALU.add).then_inc(bound_ready, 1)
            dve.wait_ge(bound_ready, 1)
            dve.tensor_copy(sq[:, 1:2], sqp[:, 8:9]).then_inc(squares_ready, 1)
            head_rows(0)
            add_attention(0, 0)
            dve.wait_ge(norm_ready, 1)
            dve.tensor_copy(bnd[:, 0:1], norm[:, 0:1]).then_inc(bound_ready, 1)
            dve.scalar_tensor_tensor(bnd[:, 1:2], gmax[:, :], 23.0, norm[:, 2:3], ALU.mult, ALU.add).then_inc(bound_ready, 1)
            dve.wait_ge(bound_ready, 3)
            dve.tensor_tensor(bnd[:, 4:5], bnd[:, 1:2], norm[:, 0:1], ALU.mult).then_inc(bound_ready, 1)
            dve.wait_ge(bound_ready, 4)
            dve.tensor_tensor(bnd[:, 2:3], bnd[:, 4:5], norm[:, 1:2], ALU.add).then_inc(bound_ready, 1)
            dve.wait_ge(bound_ready, 5)
            then = power_of_two(slice(0, 3), 0)
            then(dve.tensor_tensor(cc[:, 0:1], isc[:, 0:1], isc[:, 1:2], ALU.mult))
            then(dve.tensor_tensor(c1, cc[:, 0:1], sc[:, 2:3], ALU.mult))
            then(dve.tensor_scalar(b1S, cols[:, 0:NJ], sc[:, 2:3], None, ALU.mult))
            then(dve.tensor_scalar(colsS[:, NJ:], cols[:, NJ:], sc[:, 1:2], None, ALU.mult))
            dve.tensor_copy(cc[:, 3:4], sc[:, 0:1]).then_inc(scales_ready, 1)
            split_w1(0)
            stats(0, 0, yz, y_ready, bn_ready, mv_ready)
            split_w1(1)
            normalise(0)
            for c in range(NC):
                o1_low(0, 0, c)
            split_w1(2)
            split_w1(3)
            dve.wait_ge(addB_ready, 1)
            residual(0, 0, range(NT))
            hidden_low(0, 0)
            dve.wait_ge(w2_squares, 4)
            dve.tensor_reduce(sq[:, 2:3], sqp[:, 4:8], AX.X, ALU.add).then_inc(squares_ready, 1)
            dve.wait_ge(norm_w2, 1)
            dve.tensor_copy(bnd[:, 3:4], norm[:, 3:4]).then_inc(bound_ready, 1)
            dve.wait_ge(bound_ready, 6)
            then = power_of_two(slice(3, 4), 9)
            then(dve.tensor_tensor(c2, isc[:, 2:3], isc[:, 3:4], ALU.mult))
            dve.tensor_copy(cc[:, 3:4], sc[:, 3:4]).then_inc(w2_scale, 1)
            for q in range(4):
                dve.wait_ge(w2hi_ready, q + 1)
                dve.scalar_tensor_tensor(w2lo[:, 4 * q:4 * q + 4], w2_st[q % 2], sc[:, 3:4],
                                         w2hi[:, 4 * q:4 * q + 4], ALU.mult, ALU.subtract).then_inc(w2lo_ready, 1)

            R_AT = [0, 4, 11, 14, 21, 25, 32]

            def block_steps(b, slot, front):
                n, nslot = b + 1, 1 - slot
                last = not isinstance(b, int) or b > 0
                for j in range(NJ):
                    if front and j == 7:
                        xbar_out(n)
                    if front and j == 8:
                        head_rows(n)
                    if front and j == 9:
                        add_attention(n, nslot)
                    if front or j < NJ - 1:
                        hidden_low(NJ * b + j + 1, (j + 1) % 2)
                    if last:
                        if j == 6:
                            stats(b - 1, 1, y2, y2_ready, bn2_ready, mv2_ready)
                        if j == 7:
                            ln2(b - 1, (0, 1))
                        if j == 8:
                            ln2(b - 1, (2, 3))
                    if not front:
                        continue
                    if j == 2:
                        x_rest(n, nslot)
                    if j == 4:
                        x_part3(n)
                    if j < 6:
                        scores(n, nslot, R_AT[j], R_AT[j + 1])
                    if j == 5:
                        scores_max(n, None)
                        scores_shift(n)
                        e_parts(n)
                    if j == 10:
                        stats(n, 0, yz, y_ready, bn_ready, mv_ready)
                    if j == 11:
                        normalise(n)
                    if j in Z_AT:
                        for c in Z_AT[j]:
                            o1_low(n, nslot, c)
                    if j >= 12:
                        residual(n, nslot, (j - 12,))
                add_ffn(b, slot)

            block_steps(0, 0, True)
            with nc.vector.Fori(0, NB // 2 - 1) as i:
                for k in range(2):
                    block_steps(2 * i + 1 + k, 1 - k, True)
            block_steps(NB - 1, 1, False)
            stats(NB - 1, 1, y2, y2_ready, bn2_ready, mv2_ready)
            for t in range(NT):
                ln2(NB - 1, (t,))

        @block.tensor
        def _(te):
            def weighted_x(n):
                te.wait_ge(e_split, 3 * (n + 1))
                te.wait_ge(e1_ready, n + 1)
                te.wait_ge(x1_ready, n + 1)
                te.wait_ge(x2_ready, n + 1)
                te.wait_ge(x3_ready, n + 1)
                if not isinstance(n, int) or n > 0:
                    te.wait_ge(o1f_ready, NC * n - 1)
                W = NP * NH
                for c in range(NC):
                    for t in range(NT):
                        for g in range(NP):
                            w = (NP - g) * NH
                            te.matmul(aux[0][:, c * W:c * W + w], xp[:, g, t, c * P:(c + 1) * P],
                                      ep[:, t, 0:NP - g].rearrange("p g h -> p (g h)"),
                                      start=(t == 0 and g == 0), stop=(t == NT - 1 and g == NP - 1))
                for k in range(2):
                    for t in range(NT):
                        mm = te.matmul(aux[0][:, (NC + k) * W:(NC + k + 1) * W], masks_b[:, k],
                                       ep[:, t].rearrange("p g h -> p (g h)"), start=(t == 0), stop=(t == NT - 1))
                mm.then_inc(xbar_done, 1)

            def project_q(n, slot):
                te.wait_ge(xs_split, 5 * (n + 1))
                if not isinstance(n, int) or n > 0:
                    te.wait_ge(o1f_ready, NC * n)
                W = NP * NH
                for m in range(NC):
                    rows = slice(m * P, (m + 1) * P)
                    for g in range(NP):
                        w = (NP - g) * NH
                        for c in range(NC):
                            te.matmul(aux[1][:, m * W:m * W + w], wqp[:, g, c, rows],
                                      xsp[:, c, 0:NP - g].rearrange("p g h -> p (g h)"),
                                      start=(c == 0 and g == 0), stop=False)
                        mm = te.matmul(aux[1][:, m * W:m * W + w], peb[:, slot, g, rows],
                                       xsp[0:SPB, NC + 1, 0:NP - g].rearrange("p g h -> p (g h)"),
                                       start=False, stop=(g == NP - 1))
                mm.then_inc(o_done, 1)

            def project_out(n):
                te.wait_ge(ocx_ready, 2 * (n + 1))
                te.wait_ge(xs_ready, n + 1)
                te.matmul(aux[0][:, :], ocx[:, :, :].rearrange("p h r -> p (h r)"), wfcS[:, :],
                          start=True, stop=True).then_inc(ao_done, 1)

            def transpose_z(n, c):
                te.wait_ge(z_ready, NT * (n + 1))
                if c >= 2:
                    te.wait_ge(o1f_ready, NC * n + c - 1)
                for t in range(NT):
                    mm = te.transpose(aux[c % 2][:, t * P:(t + 1) * P], yz[:, t, c * P:(c + 1) * P], ident)
                mm.then_inc(zT_done, 1)

            def ffn1(g, j, slot):
                s = j % 2
                if not isinstance(g, int) or g >= 2:
                    te.wait_ge(hf_ready, g - 1)
                k = 0
                for c in range(NC):
                    cols_ = slice(j * P, (j + 1) * P)
                    for w, o in ((w1hi, o1hi), (w1hi, o1lo), (w1lo, o1hi)):
                        mm = te.matmul(hps[s][:, :], w[:, c, cols_], o[:, slot, c],
                                       start=(k == 0), stop=(k == 3 * NC - 1))
                        k += 1
                mm.then_inc(ffn1_done, 1)

            def ffn2(g, j, b):
                s = j % 2
                te.wait_ge(hhi_ready, g + 1)
                for t in range(NT):
                    if j == 0 and (not isinstance(b, int) or b > 0):
                        te.wait_ge(y2_ready, NT * (b - 1) + t + 1)
                    tok = slice(t * P, (t + 1) * P)
                    te.matmul(acc[t][:, :], hhi[:, s, tok], w2hi[:, j], start=(j == 0), stop=False)
                    te.matmul(acc[t][:, :], hhi[:, s, tok], w2lo[:, j], start=False, stop=False)
                te.wait_ge(hlo_ready, g + 1)
                for t in range(NT):
                    tok = slice(t * P, (t + 1) * P)
                    mm = te.matmul(acc[t][:, :], hlo[:, s, tok], w2hi[:, j], start=False, stop=(j == NJ - 1))
                mm.then_inc(ffn2_done, 1)

            te.wait_ge(dma_small, 16 * 10)
            te.wait_ge(dma_x[0], 32)
            for c in range(NC):
                for t in range(NT):
                    mm = te.transpose(acc[c][:, t * P:(t + 1) * P], xb[:, 0, t, c * P:(c + 1) * P], ident)
                mm.then_inc(xT_done, 1)
            te.wait_ge(wrc_ready, 1)
            te.wait_ge(xT_ready, NC)
            for t in range(NT):
                for c in range(NC):
                    mm = te.matmul(aux[1][:, t * NH:(t + 1) * NH], xT_st[:, c, t * P:(t + 1) * P], wr_c[:, c],
                                   start=(c == 0), stop=(c == NC - 1))
            mm.then_inc(r0_done, 1)
            te.wait_ge(masks_ready, 1)
            weighted_x(0)
            te.wait_ge(wq_split, 4)
            te.wait_ge(rmx_ready, 1)
            project_q(0, 0)
            te.wait_ge(dma_wq, 16)
            wr_banks = (hps + acc) * 2
            for h in range(NH):
                rows = slice(64 * (h % 2), 64 * (h % 2) + 64)
                if h >= 6:
                    te.wait_ge(wrB_ready, h - 5)
                te.matmul(wr_banks[h][:, :], ones[rows, :], wq_st[rows, h // 2, :],
                          start=True, stop=True).then_inc(wr_ready, 1)
            te.wait_ge(dma_wfc, 16)
            te.wait_ge(wrB_ready, 6)
            for c in range(NC):
                mm = te.matmul(acc[3][:, :], fold, wfc_st[:, c], start=(c == 0), stop=(c == NC - 1))
            mm.then_inc(wfc_ready, 1)
            te.wait_ge(wfcS_ready, 1)
            project_out(0)
            for c in range(NC):
                transpose_z(0, c)
            te.wait_ge(w1lo_ready, 1)
            te.wait_ge(o1hi_ready, NC)
            te.wait_ge(o1lo_ready, NC)
            te.wait_ge(wrB_ready, NH)
            ffn1(0, 0, 0)

            def block_steps(b, slot, front):
                n, nslot = b + 1, 1 - slot
                for j in range(NJ):
                    if front and j == NJ - 1:
                        te.wait_ge(o1hi_ready, NC * (n + 1))
                        te.wait_ge(o1lo_ready, NC * (n + 1))
                        ffn1(NJ * n, 0, nslot)
                    first = isinstance(b, int) and b == 0
                    if j < NJ - 1:
                        if first and (j + 1) % 4 == 0:
                            te.wait_ge(w1lo_ready, (j + 1) // 4 + 1)
                        ffn1(NJ * b + j + 1, j + 1, slot)
                    if front and j == 7:
                        weighted_x(n)
                    if front and j == 8:
                        project_q(n, nslot)
                    if front and j == 9:
                        project_out(n)
                    if front and j in Z_AT:
                        for c in Z_AT[j]:
                            transpose_z(n, c)
                    if first and j % 4 == 0:
                        te.wait_ge(w2lo_ready, j // 4 + 1)
                    ffn2(NJ * b + j, j, b)

            block_steps(0, 0, True)
            with nc.tensor.Fori(0, NB // 2 - 1) as i:
                for k in range(2):
                    block_steps(2 * i + 1 + k, 1 - k, True)
            block_steps(NB - 1, 1, False)


def kernel(x, L0_conv_Wq, L0_conv_Wfc, L0_conv_W1, L0_conv_b1, L0_conv_W2, L0_conv_b2,
           L0_conv_g1, L0_conv_be1, L0_conv_g2, L0_conv_be2):
    import numpy as np
    import concourse.bacc as bacc
    from concourse.bass_utils import run_bass_kernel_spmd

    S = x.shape[0]
    pos = np.arange(S, dtype=np.float32)[:, None]
    div = np.exp(np.arange(0, D, 2, dtype=np.float32) * np.float32(-np.log(10000.0) / D)).astype(np.float32)
    ang = (pos * div).astype(np.float32)
    pe = np.zeros((S, D), np.float32)
    pe[:, 0::2] = np.sin(ang)
    pe[:, 1::2] = np.cos(ang)
    parts, rest = [], pe
    for _ in range(NP):
        cut = (rest.view(np.uint32) & np.uint32(0xFFFF0000)).view(np.float32)
        parts.append((cut.view(np.uint32) >> 16).astype(np.uint16))
        rest = rest - cut
    pr = pe.reshape(NB, SPB, NH, DEPTH).sum(-1, dtype=np.float64).astype(np.float32)
    p = np.arange(P)
    pe_r = np.ascontiguousarray(pr[:, p // 4, :].transpose(1, 0, 2).reshape(P, NB * NH))
    masks = np.concatenate([np.eye(P), (p[:, None] % 64 == p[None, :] % 64), np.ones((P, P)),
                            (p[:, None] // 4 == p[None, :])], axis=1).astype(np.float32)
    arrays = {
        "x": np.ascontiguousarray(x).reshape(-1, D),
        "wq": np.ascontiguousarray(L0_conv_Wq),
        "wqT": np.ascontiguousarray(np.asarray(L0_conv_Wq).T),
        "wfcT": np.ascontiguousarray(np.asarray(L0_conv_Wfc).T),
        "w1T": np.ascontiguousarray(np.asarray(L0_conv_W1).T),
        "b1": np.ascontiguousarray(L0_conv_b1),
        "w2T": np.ascontiguousarray(np.asarray(L0_conv_W2).T),
        "b2": np.ascontiguousarray(L0_conv_b2),
        "g1": np.ascontiguousarray(L0_conv_g1),
        "be1": np.ascontiguousarray(L0_conv_be1),
        "g2": np.ascontiguousarray(L0_conv_g2),
        "be2": np.ascontiguousarray(L0_conv_be2),
        "pe_parts": np.ascontiguousarray(np.stack(parts, axis=1)),
        "pe_r": pe_r,
        "masks": masks,
    }
    nc = bacc.Bacc("TRN2", target_bir_lowering=False, num_devices=1)
    args = [nc.dram_tensor(f"in_{k}", a.shape, mybir.dt.from_np(a.dtype), kind="ExternalInput").ap() for k, a in arrays.items()]
    out = nc.dram_tensor("out_y", (NB * TB, D), mybir.dt.float32, kind="ExternalOutput").ap()
    conv_seq_kernel(nc, *args, out)
    r = run_bass_kernel_spmd(nc, [{f"in_{k}": a for k, a in arrays.items()}], core_ids=[0])
    return r.results[0]["out_y"].reshape(x.shape)
```

```python
import concourse.bass as bass
from concourse import mybir
from contextlib import ExitStack

D = 512
DFF = 2048
NH = 8
DEPTH = D // NH
TB = 512
NB = 16
P = 128
NT = TB // P
NC = D // P
NP = 3
NJ = DFF // P
SPB = TB // 16
EPS = 1e-5
Z_AT = {12: (0, 1), 13: (2, 3)}


def conv_seq_kernel(nc, x, wqT, wfc, w1T, w2T, b2, g1, be1, g2, be2, cols_in, pe_parts, pe_r, masks, out):
    f32 = mybir.dt.float32
    f16 = mybir.dt.float16
    bf16 = mybir.dt.bfloat16
    u32 = mybir.dt.uint32
    ALU = mybir.AluOpType
    ACT = mybir.ActivationFunctionType
    AX = mybir.AxisListType

    x_v = x.rearrange("(b p t) f -> b p (t f)", p=P, t=NT)
    out_v = out.rearrange("(b p t) f -> b p (t f)", p=P, t=NT)
    pe_v = pe_parts.rearrange("(b s) g f -> b s g f", s=SPB).bitcast(bf16)
    w1_v = w1T.rearrange("(c p) (q n) -> q p c n", p=P, q=4)
    w2_v = w2T.rearrange("(q j p) n -> q p j n", p=P, q=4)

    ctx = ExitStack()
    with ctx:
        def sb(name, shape, dt=f32):
            return ctx.enter_context(nc.sbuf_tensor(name, shape, dt))

        def pb(name):
            return ctx.enter_context(nc.psum_tensor(name, [P, 512], f32))

        def sem(name):
            return ctx.enter_context(nc.semaphore(name))

        w1hi = sb("w1hi", [P, NC, DFF], f16)
        w1lo = sb("w1lo", [P, NC, DFF], f16)
        w2 = sb("w2", [P, 2, NJ, D], f16)
        w2hi, w2lo = w2[:, 0], w2[:, 1]
        wqp = sb("wqp", [P, NP, NC, D], bf16)
        wrB = sb("wrB", [P, NH, D])
        wfcS = sb("wfcS", [P, D])
        g1B = sb("g1B", [P, D])
        addB = sb("addB", [P, D])
        g2B = sb("g2B", [P, D])
        be2B = sb("be2B", [P, D])
        masks_sb = sb("masks_sb", [P, 3 * P])
        ident = masks_sb[:, 0:P]
        masks_b = sb("masks_b", [P, 2, P], bf16)
        peR = sb("peR", [P, NB, NH])
        cols = sb("cols", [P, NJ + 2 * NC])
        colsS = sb("colsS", [P, NJ + 2 * NC])
        b1S = colsS[:, 0:NJ]
        g1S = colsS[:, NJ:NJ + NC]
        be1S = colsS[:, NJ + NC:NJ + 2 * NC]
        xb = sb("xb", [P, 2, NT, D])
        peb = sb("peb", [SPB, 2, NP, D], bf16)
        xp = sb("xp", [P, NP, NT, D], bf16)
        yz = sb("yz", [P, NT, D])
        o1b = sb("o1b", [P, 2, NT, D])
        y2 = sb("y2", [P, NT, D])
        o1f = sb("o1f", [P, 2, TB])
        o1 = sb("o1", [P, 2, 2, NC, TB], f16)
        o1hi, o1lo = o1[:, :, 0], o1[:, :, 1]
        hf = sb("hf", [P, 2, TB])
        hhi = sb("hhi", [P, 2, TB], f16)
        hlo = sb("hlo", [P, 2, TB], f16)
        scr = sb("scr", [P, 2, D])
        rr = sb("rr", [P, NT, NH])
        rp = sb("rp", [P, NT, NH])
        rs = sb("rs", [P, NT, NH])
        ee = sb("ee", [P, NT, NH])
        ep = sb("ep", [P, NT, NP, NH], bf16)
        rmx = sb("rmx", [P, NH])
        mxB = sb("mxB", [P, NH])
        xs = sb("xs", [P, NC + 2, NH])
        xsp = sb("xsp", [P, NC + 2, NP, NH], bf16)
        osum = sb("osum", [P, NC])
        rden = sb("rden", [P, NH])
        ocx = sb("ocx", [P, NH, 16])
        bn = sb("bn", [P, 2, NT, 6])
        mv = sb("mv", [P, 2, NT, 2])
        var_eps = sb("var_eps", [P, 2, NT])
        rstd = sb("rstd", [P, 2, NT])
        half = sb("half", [P, 2, NT])
        wr_c = sb("wr_c", [P, NC, NH])
        sqp = sb("sqp", [P, 9])
        sq = sb("sq", [P, 4])
        norm2 = sb("norm2", [P, 4])
        norm = sb("norm", [P, 4])
        gmax = sb("gmax", [P, 1])
        bnd = sb("bnd", [P, 6])
        pw = sb("pw", [P, 4])
        sc = sb("sc", [P, 4])
        isc = sb("isc", [P, 4])
        cc = sb("cc", [P, 4])
        c1 = cc[:, 1:2]
        c2 = cc[:, 2:3]

        w1_st = w2[:, :, :, :].rearrange("p a j n -> p (a j n)").bitcast(f32).rearrange(
            "p (q c n) -> p q c n", q=4, c=NC)
        W1_PLACE = (0, 2, 1, 3)
        in_w1hi = w1hi[:, :, :].rearrange("p c n -> p (c n)").bitcast(f32)
        in_w1lo = w1lo[:, :, :].rearrange("p c n -> p (c n)").bitcast(f32)
        xT_st = in_w1hi[:, 0:NC * TB].rearrange("p (c n) -> p c n", c=NC)
        wqT_st = in_w1lo[:, 0:NC * D].rearrange("p (c n) -> p c n", c=NC)
        wfc_st = in_w1lo[:, NC * D:2 * NC * D].rearrange("p (c n) -> p c n", c=NC)
        wfcF = scr[:, 1].rearrange("p (c a k) -> p c a k", c=NC, a=2)
        o1_slot1 = o1[:, 1].rearrange("p a c n -> p (a c n)").bitcast(f32).rearrange("p (j n) -> p j n", j=NC)
        w2_st = [y2[:, :, :], o1_slot1, o1b[:, 1], o1b[:, 0]]
        w2_split_st = w2_st[0:3] + [y2[:, :, :]]
        be1_st = o1f[:, 0, :]
        b2_st = o1f[:, 1, :]

        acc = [pb(f"acc{t}") for t in range(NT)]
        hps = [pb(f"hps{t}") for t in range(2)]
        aux = [pb(f"aux{t}") for t in range(2)]
        wr_banks = (hps + acc[0:3]) + (hps + acc[0:1])

        dma_x = [sem("dma_x0"), sem("dma_x1")]
        dma_masks, dma_peR, dma_small, dma_rows = sem("dma_masks"), sem("dma_peR"), sem("dma_small"), sem("dma_rows")
        dma_wqT, dma_wfc = sem("dma_wqT"), sem("dma_wfc")
        dma_w1 = [sem(f"dma_w1_{q}") for q in range(4)]
        dma_w2 = [sem(f"dma_w2_{q}") for q in range(4)]
        dma_w2_again = sem("dma_w2_again")
        dma_out = sem("dma_out")
        wr_ready, wrB_ready = sem("wr_ready"), sem("wrB_ready")
        wfcF_ready, wfc_ready, wfcS_ready = sem("wfcF_ready"), sem("wfc_ready"), sem("wfcS_ready")
        consts_set, masks_ready = sem("consts_set"), sem("masks_ready")
        xT_done, xT_ready, wrc_ready, r0_done = sem("xT_done"), sem("xT_ready"), sem("wrc_ready"), sem("r0_done")
        wq_split = sem("wq_split")
        w1_squares, w2_squares, w2_last_squares = sem("w1_squares"), sem("w2_squares"), sem("w2_last_squares")
        squares_ready, small_ready = sem("squares_ready"), sem("small_ready")
        norm2_ready, norm_ready, norm2_w2, norm_w2 = sem("norm2_ready"), sem("norm_ready"), sem("norm2_w2"), sem("norm_w2")
        bound_ready, scale_step, scales_ready = sem("bound_ready"), sem("scale_step"), sem("scales_ready")
        w2_scale = sem("w2_scale")
        w1hi_ready, w1lo_ready, w2hi_ready, w2lo_ready = sem("w1hi_ready"), sem("w1lo_ready"), sem("w2hi_ready"), sem("w2lo_ready")
        x1_ready, d1_ready, x2_ready, x3_ready = sem("x1_ready"), sem("d1_ready"), sem("x2_ready"), sem("x3_ready")
        addB_ready = sem("addB_ready")
        ffn1_done, ffn2_done, last_acc_done = sem("ffn1_done"), sem("ffn2_done"), sem("last_acc_done")
        hhi_ready, hf_ready, hlo_ready = sem("hhi_ready"), sem("hf_ready"), sem("hlo_ready")
        r_ready, rp_ready, rmx_ready, mx_ready, rs_ready = sem("r_ready"), sem("rp_ready"), sem("rmx_ready"), sem("mx_ready"), sem("rs_ready")
        e_ready, e1_ready, e_split = sem("e_ready"), sem("e1_ready"), sem("e_split")
        xbar_done, xs_ready, xs_split, rden_ready = sem("xbar_done"), sem("xs_ready"), sem("xs_split"), sem("rden_ready")
        osum_ready = sem("osum_ready")
        o_done, ocx_ready, ao_done = sem("o_done"), sem("ocx_ready"), sem("ao_done")
        y_ready, bn_ready, mv_ready, z_ready, zT_done = sem("y_ready"), sem("bn_ready"), sem("mv_ready"), sem("z_ready"), sem("zT_done")
        var_ready, rstd_ready = [sem("var1_ready"), sem("var2_ready")], [sem("rstd1_ready"), sem("rstd2_ready")]
        o1hi_ready, o1f_ready, o1lo_ready = sem("o1hi_ready"), sem("o1f_ready"), sem("o1lo_ready")
        o1g_ready, o1b_ready = sem("o1g_ready"), sem("o1b_ready")
        y2_ready, bn2_ready, mv2_ready = sem("y2_ready"), sem("bn2_ready"), sem("mv2_ready")
        z2g_ready, out_ready = sem("z2g_ready"), sem("out_ready")

        dve_passed, pool_passed = sem("dve_passed"), sem("pool_passed")

        block = ctx.enter_context(nc.Block())

        def x_loaded(n, slot):
            return 16 * (n - slot) + 32

        @block.sync
        def _(sp):
            def load_x(b, slot):
                sp.dma_start(xb[:, slot].rearrange("p t f -> p (t f)"), x_v[b]).then_inc(dma_x[slot], 16)
                sp.dma_start(peb[:, slot], pe_v[b]).then_inc(dma_x[slot], 16)

            sp.dma_start(wqT_st, wqT.rearrange("(c p) n -> p c n", p=P)).then_inc(dma_wqT, 16)
            load_x(0, 0)
            sp.dma_start(wfc_st, wfc.rearrange("(c p) n -> p c n", p=P)).then_inc(dma_wfc, 16)
            for q in range(4):
                sp.dma_start(w1_st[:, W1_PLACE[q]], w1_v[q]).then_inc(dma_w1[q], 16)
            for q in range(4):
                sp.dma_start(w2_st[q], w2_v[q]).then_inc(dma_w2[q], 16)
            load_x(1, 1)
            sp.wait_ge(w2hi_ready, 1)
            sp.wait_ge(w2lo_ready, 1)
            sp.dma_start(w2_split_st[3], w2_v[3]).then_inc(dma_w2_again, 16)

            def next_x(n, slot):
                sp.wait_ge(y_ready, NT * (n - 1))
                load_x(n, slot)

            def store(b):
                sp.wait_ge(out_ready, NT * (b + 1))
                sp.dma_start(out_v[b], y2[:, :, :].rearrange("p t f -> p (t f)")).then_inc(dma_out, 16)

            next_x(2, 0)
            next_x(3, 1)
            with nc.sync.Fori(0, NB // 2 - 2) as i:
                for par in range(2):
                    store(2 * i + par)
                    next_x(2 * i + par + 4, par)
            for b in range(NB - 4, NB - 1):
                store(b)
            for t in range(NT):
                sp.wait_ge(out_ready, NT * (NB - 1) + t + 1)
                sp.dma_start(out_v[NB - 1][:, t * D:(t + 1) * D], y2[:, t]).then_inc(dma_out, 16)
            sp.wait_ge(dma_out, 16 * (NB - 1 + NT))

        @block.gpsimd
        def _(pool):
            RMAX = bass.bass_isa.ReduceOp.max
            RADD = bass.bass_isa.ReduceOp.add
            pool.memset(half[:, 0], -0.5).then_inc(consts_set, 1)
            pool.memset(half[:, 1], 0.5).then_inc(consts_set, 1)
            pool.memset(ocx[:, :, :], 0.0).then_inc(consts_set, 1)

            def passed():
                pool.sem_inc(pool_passed, 1)

            def token_max(n):
                if not isinstance(n, int) or n > 0:
                    pool.wait_ge(rs_ready, n)
                pool.wait_ge(rmx_ready, n + 1)
                passed()
                pool.partition_all_reduce(mxB[:, :], rmx[:, :], P, RMAX).then_inc(mx_ready, 1)

            def inv_std(k, mv_sem, n):
                pool.wait_ge(mv_sem, NT * (n + 1))
                passed()
                pool.tensor_scalar(var_eps[:, k], mv[:, k, :, 1], EPS, None, ALU.add).then_inc(var_ready[k], 1)
                pool.wait_ge(var_ready[k], n + 1)
                pool.tensor_tensor(rstd[:, k], var_eps[:, k], half[:, 0], ALU.pow).then_inc(rstd_ready[k], 1)

            pool.wait_ge(consts_set, 3)
            token_max(0)
            pool.wait_ge(squares_ready, 1)
            pool.partition_all_reduce(norm2[:, 0:2], sq[:, 0:2], P, RADD).then_inc(norm2_ready, 1)
            pool.wait_ge(norm2_ready, 1)
            pool.wait_ge(small_ready, 2)
            pool.tensor_tensor(norm[:, 0:3], norm2[:, 0:3], half[:, 1, 0:3], ALU.pow).then_inc(norm_ready, 1)
            inv_std(0, mv_ready, 0)
            pool.wait_ge(squares_ready, 2)
            pool.partition_all_reduce(norm2[:, 3:4], sq[:, 2:3], P, RADD).then_inc(norm2_w2, 1)
            pool.wait_ge(norm2_w2, 1)
            pool.tensor_tensor(norm[:, 3:4], norm2[:, 3:4], half[:, 1, 0:1], ALU.pow).then_inc(norm_w2, 1)
            pool.wait_ge(dma_small, 16 * 3)
            pool.wait_ge(addB_ready, 1)
            pool.wait_ge(w2_last_squares, 1)
            for t in range(NT):
                pool.wait_ge(z_ready, t + 1)
                pool.tensor_tensor(o1b[:, 0, t], yz[:, t], g1B[:, :], ALU.mult).then_inc(o1g_ready, 1)
            for t in range(NT):
                pool.wait_ge(o1g_ready, t + 1)
                pool.tensor_tensor(o1b[:, 0, t], o1b[:, 0, t], addB[:, :], ALU.add).then_inc(o1b_ready, 1)
            token_max(1)
            inv_std(0, mv_ready, 1)

            with nc.gpsimd.Fori(0, NB // 2 - 1) as i:
                for k in range(2):
                    b = 2 * i + 1 + k
                    token_max(b + 1)
                    inv_std(1, mv2_ready, b - 1)
                    inv_std(0, mv_ready, b + 1)
            inv_std(1, mv2_ready, NB - 2)
            for t in range(NT):
                pool.wait_ge(mv2_ready, NT * (NB - 1) + t + 1)
                pool.tensor_scalar(var_eps[:, 1, t:t + 1], mv[:, 1, t, 1:2], EPS, None, ALU.add).then_inc(var_ready[1], 1)
                pool.wait_ge(var_ready[1], NB + t)
                pool.tensor_tensor(rstd[:, 1, t:t + 1], var_eps[:, 1, t:t + 1], half[:, 0, 0:1],
                                   ALU.pow).then_inc(rstd_ready[1], 1)

        @block.scalar
        def _(act):
            act.dma_start(masks_sb[:, :], masks).then_inc(dma_masks, 16)
            act.dma_start(cols[:, :], cols_in).then_inc(dma_small, 16)
            act.dma_start(peR[:, :, :], pe_r.rearrange("p (b h) -> p b h", b=NB)).then_inc(dma_peR, 16)
            for dst, src, done in ((g1B[:, :], g1, dma_small), (be1_st, be1, dma_small), (b2_st, b2, dma_rows),
                                   (g2B[:, :], g2, dma_rows), (be2B[:, :], be2, dma_rows)):
                act.dma_start(dst, src.unsqueeze(0).broadcast_to([P, D])).then_inc(done, 16)

            def exp_scores(n):
                act.wait_ge(rs_ready, n + 1)
                if not isinstance(n, int) or n > 0:
                    act.wait_ge(xbar_done, n)
                    act.wait_ge(e_split, 3 * n)
                act.activation(ee[:, :, :], rs[:, :, :], ACT.Exp).then_inc(e_ready, 1)
                act.activation(ep[:, :, 0], rs[:, :, :], ACT.Exp).then_inc(e1_ready, 1)

            def x_part1(n, slot):
                if not isinstance(n, int) or n > 0:
                    act.wait_ge(xbar_done, n)
                act.wait_ge(dma_x[slot], x_loaded(n, slot))
                act.activation(xp[:, 0], xb[:, slot], ACT.Copy).then_inc(x1_ready, 1)

            def x_part2(n):
                act.wait_ge(d1_ready, n + 1)
                act.activation(xp[:, 1], yz[:, :, :], ACT.Copy).then_inc(x2_ready, 1)

            def o1_chunk(n, slot, c):
                act.wait_ge(zT_done, NC * n + c + 1)
                act.activation(o1hi[:, slot, c], aux[c % 2][:, :], ACT.Identity,
                               bias=be1S[:, c:c + 1], scale=g1S[:, c:c + 1]).then_inc(o1hi_ready, 1)
                if c >= 2 or not isinstance(n, int) or n > 0:
                    act.wait_ge(o1lo_ready, NC * n + c - 1)
                act.activation(o1f[:, c % 2], aux[c % 2][:, :], ACT.Identity,
                               bias=be1S[:, c:c + 1], scale=g1S[:, c:c + 1]).then_inc(o1f_ready, 1)

            def hidden(g, j):
                s = j % 2
                act.wait_ge(ffn1_done, g + 1)
                if not isinstance(g, int) or g >= 2:
                    act.wait_ge(ffn2_done, g - 1)
                act.activation(hhi[:, s], hps[s][:, :], ACT.Relu,
                               bias=b1S[:, j:j + 1], scale=c1).then_inc(hhi_ready, 1)
                if not isinstance(g, int) or g >= 2:
                    act.wait_ge(hlo_ready, g - 1)
                act.activation(hf[:, s], hps[s][:, :], ACT.Relu,
                               bias=b1S[:, j:j + 1], scale=c1).then_inc(hf_ready, 1)

            x_part1(0, 0)
            for c in range(NC):
                act.wait_ge(xT_done, c + 1)
                act.activation(xT_st[:, c], acc[c][:, :], ACT.Copy).then_inc(xT_ready, 1)
            squares = hf[:, :, :].rearrange("p a n -> p (a n)").bitcast(bf16).rearrange("p (c n) -> p c n", c=NC)

            def sum_squares(src, k, done):
                if 0 < k:
                    act.wait_ge(w1_squares, min(k, 4))
                if k > 4:
                    act.wait_ge(w2_squares, k - 4)
                act.activation(squares, src, ACT.Square, accum_out=sqp[:, k:k + 1]).then_inc(done, 1)

            def copy_wr(h):
                act.wait_ge(wr_ready, h + 1)
                act.activation(wrB[:, h], wr_banks[h][:, :], ACT.Copy).then_inc(wrB_ready, 1)

            def high_w1(q):
                act.activation(w1hi[:, :, q * D:(q + 1) * D], w1_st[:, W1_PLACE[q]], ACT.Copy,
                               scale=sc[:, 0:1]).then_inc(w1hi_ready, 1)

            def high_w2(q):
                act.wait_ge(w1lo_ready, 1 if q < 2 else 3)
                if q == 3:
                    act.wait_ge(dma_w2_again, 16)
                act.activation(w2hi[:, 4 * q:4 * q + 4], w2_split_st[q], ACT.Copy,
                               scale=sc[:, 3:4]).then_inc(w2hi_ready, 1)

            def squares_w1(q):
                act.wait_ge(dma_w1[q], 16)
                sum_squares(w1_st[:, W1_PLACE[q]], q, w1_squares)

            def squares_w2(q):
                act.wait_ge(dma_w2[q], 16)
                sum_squares(w2_st[q], 4 + q, w2_squares)

            x_part2(0)
            squares_w1(0)
            squares_w1(1)
            exp_scores(0)
            for h in range(4):
                copy_wr(h)
            squares_w1(2)
            squares_w1(3)
            act.wait_ge(dma_small, 16 * 3)
            act.activation(colsS[:, 0:NJ], cols[:, 0:NJ], ACT.Square, accum_out=sqp[:, 8:9]).then_inc(w1_squares, 1)
            act.wait_ge(wfc_ready, 1)
            act.activation(wfcS[:, :], acc[3][:, :], ACT.Copy).then_inc(wfcS_ready, 1)
            squares_w2(0)
            for h in range(4, NH):
                copy_wr(h)
            act.wait_ge(r0_done, 1)
            act.wait_ge(scales_ready, 1)
            high_w1(0)
            squares_w2(1)
            high_w1(1)
            squares_w2(2)
            for c in range(NC):
                o1_chunk(0, 0, c)
            act.wait_ge(w2_scale, 1)
            high_w2(0)
            act.wait_ge(w2_squares, 3)
            hidden(0, 0)

            def block_steps(b, slot, front):
                first = isinstance(b, int) and b == 0
                for j in range(NJ):
                    if front or j < NJ - 1:
                        hidden(NJ * b + j + 1, (j + 1) % NJ)
                    if not front:
                        continue
                    if j == 0:
                        x_part1(b + 1, 1 - slot)
                    if j == 3:
                        x_part2(b + 1)
                    if j == 5 + first:
                        exp_scores(b + 1)
                    if first:
                        if j == 0:
                            high_w2(1)
                        if j in (1, 2):
                            high_w1(j + 1)
                        if j in (7, 9):
                            high_w2((j - 3) // 2)
                        if j == 11:
                            act.wait_ge(w2lo_ready, 2)
                    if j in Z_AT:
                        for c in Z_AT[j]:
                            o1_chunk(b + 1, 1 - slot, c)

            block_steps(0, 0, True)
            with nc.scalar.Fori(0, NB // 2 - 1) as i:
                for k in range(2):
                    block_steps(2 * i + 1 + k, 1 - k, True)
            block_steps(NB - 1, 1, False)

        @block.vector
        def _(dve):
            def scores(n, slot, lo, hi):
                if lo == 0:
                    dve.wait_ge(dma_x[slot], x_loaded(n, slot))
                for i in range(lo, hi):
                    t, h = i // NH, i % NH
                    if i >= 2 or not isinstance(n, int) or n > 1:
                        dve.wait_ge(r_ready, NT * NH * (n - 1) + i - 1)
                    dve.scalar_tensor_tensor(scr[:, i % 2], xb[:, slot, t], 1.0, wrB[:, h], ALU.mult, ALU.mult,
                                             accum_out=rr[:, t, h:h + 1]).then_inc(r_ready, 1)

            def scores_max(n, r):
                if r is None:
                    dve.wait_ge(r_ready, NT * NH * n)
                    r = rr[:, :, :]
                dve.tensor_tensor(rp[:, :, :], r, peR[:, n, :].unsqueeze(1).broadcast_to([P, NT, NH]),
                                  ALU.add).then_inc(rp_ready, 1)
                dve.wait_ge(rp_ready, n + 1)
                dve.tensor_reduce(rmx[:, :], rp[:, :, :].rearrange("p t h -> p h t"), AX.X,
                                  ALU.max).then_inc(rmx_ready, 1)

            def scores_shift(n):
                dve.wait_ge(mx_ready, n + 1)
                if not isinstance(n, int) or n > 0:
                    dve.wait_ge(e_ready, n)
                dve.tensor_tensor(rs[:, :, :], rp[:, :, :], mxB[:, :].unsqueeze(1).broadcast_to([P, NT, NH]),
                                  ALU.subtract).then_inc(rs_ready, 1)

            def x_rest(n, slot):
                dve.wait_ge(x1_ready, n + 1)
                if not isinstance(n, int) or n > 0:
                    dve.wait_ge(zT_done, NC * n)
                    dve.wait_ge(o1b_ready, NT * n)
                dve.tensor_tensor(yz[:, :, :], xb[:, slot], xp[:, 0], ALU.subtract).then_inc(d1_ready, 1)

            def x_part3(n):
                if not isinstance(n, int) or n > 0:
                    dve.wait_ge(xbar_done, n)
                dve.wait_ge(x2_ready, n + 1)
                dve.wait_ge(d1_ready, n + 1)
                dve.tensor_tensor(xp[:, 2], yz[:, :, :], xp[:, 1], ALU.subtract).then_inc(x3_ready, 1)

            def e_parts(n):
                dve.wait_ge(e_ready, n + 1)
                dve.wait_ge(e1_ready, n + 1)
                dve.tensor_tensor(ee[:, :, :], ee[:, :, :], ep[:, :, 0], ALU.subtract).then_inc(e_split, 1)
                dve.wait_ge(e_split, 3 * n + 1)
                dve.tensor_copy(ep[:, :, 1], ee[:, :, :]).then_inc(e_split, 1)
                dve.wait_ge(e_split, 3 * n + 2)
                dve.tensor_tensor(ep[:, :, 2], ee[:, :, :], ep[:, :, 1], ALU.subtract).then_inc(e_split, 1)

            def xbar_out(n):
                dve.wait_ge(xbar_done, n + 1)
                if not isinstance(n, int) or n > 0:
                    dve.wait_ge(o_done, n)
                dve.tensor_reduce(xs[:, :, :], aux[0][:, 0:(NC + 2) * NP * NH].rearrange(
                    "p (k g h) -> p k h g", k=NC + 2, g=NP), AX.X, ALU.add).then_inc(xs_ready, 1)
                dve.wait_ge(xs_ready, n + 1)
                dve.tensor_copy(xsp[:, :, 0], xs[:, :, :]).then_inc(xs_split, 1)
                dve.reciprocal(rden[:, :], xs[:, NC]).then_inc(rden_ready, 1)
                dve.wait_ge(xs_split, 5 * n + 1)
                dve.wait_ge(rden_ready, n + 1)
                dve.tensor_tensor(xs[:, :, :], xs[:, :, :], xsp[:, :, 0], ALU.subtract).then_inc(xs_split, 1)
                dve.wait_ge(xs_split, 5 * n + 2)
                dve.tensor_copy(xsp[:, :, 1], xs[:, :, :]).then_inc(xs_split, 1)
                dve.wait_ge(xs_split, 5 * n + 3)
                dve.tensor_tensor(xsp[:, :, 2], xs[:, :, :], xsp[:, :, 1], ALU.subtract).then_inc(xs_split, 2)

            def head_rows(n):
                dve.wait_ge(o_done, n + 1)
                for odd in range(2):
                    rows = slice(64 * odd, 64 * odd + 64)
                    src = aux[1][rows, 0:NC * 26].rearrange("p (m k) -> p m k", k=26)[:, :, odd:odd + 17:8]
                    dve.tensor_reduce(osum[rows, :], src, AX.X, ALU.add).then_inc(osum_ready, 1)
                if isinstance(n, int) and n == 0:
                    dve.wait_ge(consts_set, 3)
                else:
                    dve.wait_ge(ao_done, n)
                for odd in range(2):
                    rows = slice(64 * odd, 64 * odd + 64)
                    heads = slice(odd, NH, 2)
                    dve.wait_ge(osum_ready, 2 * n + odd + 1)
                    dve.tensor_tensor(ocx[rows, heads, :], osum[rows, :].unsqueeze(2).broadcast_to([64, NC, 16]),
                                      rden[rows, heads].unsqueeze(2).broadcast_to([64, NC, 16]),
                                      ALU.mult).then_inc(ocx_ready, 1)

            def add_attention(n, slot):
                dve.wait_ge(ao_done, n + 1)
                dve.wait_ge(x2_ready, n + 1)
                dve.wait_ge(x3_ready, n + 1)
                for t in range(NT):
                    dve.tensor_tensor(yz[:, t], xb[:, slot, t], aux[0][:, :], ALU.add).then_inc(y_ready, 1)

            def stats(n, k, src, src_sem, bn_sem, mv_sem):
                for t in range(NT):
                    dve.wait_ge(src_sem, NT * n + t + 1)
                    dve.bn_stats(bn[:, k, t], src[:, t]).then_inc(bn_sem, 1)
                for t in range(NT):
                    dve.wait_ge(bn_sem, NT * n + t + 1)
                    dve.sem_inc(dve_passed, 1)
                    dve.bn_aggr(mv[:, k, t], bn[:, k, t]).then_inc(mv_sem, 1)

            def normalise(n):
                dve.wait_ge(rstd_ready[0], n + 1)
                for t in range(NT):
                    dve.tensor_scalar(yz[:, t], yz[:, t], mv[:, 0, t, 0:1], rstd[:, 0, t:t + 1],
                                      ALU.subtract, ALU.mult).then_inc(z_ready, 1)

            def o1_low(n, slot, c):
                dve.wait_ge(o1f_ready, NC * n + c + 1)
                dve.wait_ge(o1hi_ready, NC * n + c + 1)
                dve.tensor_tensor(o1lo[:, slot, c], o1f[:, c % 2], o1hi[:, slot, c],
                                  ALU.subtract).then_inc(o1lo_ready, 1)

            def hidden_low(g, s):
                dve.wait_ge(hf_ready, g + 1)
                dve.wait_ge(hhi_ready, g + 1)
                if not isinstance(g, int) or g >= 2:
                    dve.wait_ge(ffn2_done, g - 1)
                dve.tensor_tensor(hlo[:, s], hf[:, s], hhi[:, s], ALU.subtract).then_inc(hlo_ready, 1)

            def residual(n, slot, ts):
                for t in ts:
                    dve.wait_ge(z_ready, NT * n + t + 1)
                    dve.tensor_tensor(o1b[:, slot, t], yz[:, t], g1B[:, :], ALU.mult).then_inc(o1g_ready, 1)
                for t in ts:
                    dve.wait_ge(o1g_ready, NT * n + t + 1)
                    dve.tensor_tensor(o1b[:, slot, t], o1b[:, slot, t], addB[:, :], ALU.add).then_inc(o1b_ready, 1)

            def ln2(b, ts):
                dve.wait_ge(rstd_ready[1], b + 1)
                for t in ts:
                    dve.scalar_tensor_tensor(y2[:, t], y2[:, t], mv[:, 1, t, 0:1], g2B[:, :],
                                             ALU.subtract, ALU.mult).then_inc(z2g_ready, 1)
                for t in ts:
                    dve.wait_ge(z2g_ready, NT * b + t + 1)
                    dve.scalar_tensor_tensor(y2[:, t], y2[:, t], rstd[:, 1, t:t + 1], be2B[:, :],
                                             ALU.mult, ALU.add).then_inc(out_ready, 1)

            def add_ffn(b, slot):
                dve.wait_ge(ffn2_done, NJ * (b + 1))
                dve.wait_ge(o1b_ready, NT * (b + 1))
                if not isinstance(b, int) or b > 0:
                    dve.wait_ge(dma_out, 16 * b)
                for t in range(NT):
                    dve.scalar_tensor_tensor(y2[:, t], acc[t][:, :], c2, o1b[:, slot, t],
                                             ALU.mult, ALU.add).then_inc(y2_ready, 1)

            def power_of_two(cols_, first):
                step = [first]

                def then(ins):
                    step[0] += 1
                    ins.then_inc(scale_step, 1)
                    dve.wait_ge(scale_step, step[0])

                then(dve.tensor_scalar(bnd[:, cols_], bnd[:, cols_], 1e-30, None, ALU.max))
                then(dve.tensor_scalar(pw[:, cols_].bitcast(u32), bnd[:, cols_].bitcast(u32), 0x7F800000, None,
                                       ALU.bitwise_and))
                then(dve.tensor_scalar(sc[:, cols_].bitcast(u32), pw[:, cols_].bitcast(u32), 0x7F800000, None,
                                       ALU.bitwise_xor))
                then(dve.tensor_scalar(sc[:, cols_], sc[:, cols_], 2.0 ** 13, None, ALU.mult))
                then(dve.tensor_scalar(isc[:, cols_], pw[:, cols_], 2.0 ** -14, None, ALU.mult))
                return then

            def low_w1(q):
                cols_ = slice(q * D, (q + 1) * D)
                dve.wait_ge(w1hi_ready, q + 1)
                dve.scalar_tensor_tensor(w1lo[:, :, cols_], w1_st[:, W1_PLACE[q]], sc[:, 0:1], w1hi[:, :, cols_],
                                         ALU.mult, ALU.subtract).then_inc(w1lo_ready, 1)

            def low_w2(q):
                dve.wait_ge(w1lo_ready, 2 if q < 2 else 4)
                dve.wait_ge(w2hi_ready, q + 1)
                dve.scalar_tensor_tensor(w2lo[:, 4 * q:4 * q + 4], w2_split_st[q], sc[:, 3:4],
                                         w2hi[:, 4 * q:4 * q + 4], ALU.mult, ALU.subtract).then_inc(w2lo_ready, 1)

            dve.wait_ge(dma_wqT, 16)
            dve.tensor_reduce(wr_c[:, :, :], wqT_st.rearrange("p c (h k) -> p c h k", h=NH), AX.X,
                              ALU.add).then_inc(wrc_ready, 1)
            dve.tensor_copy(wqp[:, 0], wqT_st).then_inc(wq_split, 1)
            dve.wait_ge(wq_split, 1)
            dve.tensor_tensor(wqT_st, wqT_st, wqp[:, 0], ALU.subtract).then_inc(wq_split, 1)
            x_rest(0, 0)
            dve.wait_ge(wq_split, 2)
            dve.tensor_copy(wqp[:, 1], wqT_st).then_inc(wq_split, 1)
            dve.wait_ge(wq_split, 3)
            dve.tensor_tensor(wqp[:, 2], wqT_st, wqp[:, 1], ALU.subtract).then_inc(wq_split, 1)
            x_part3(0)
            dve.wait_ge(r0_done, 1)
            dve.wait_ge(dma_peR, 16)
            scores_max(0, aux[1][:, 0:NT * NH].rearrange("p (t h) -> p t h", t=NT))
            dve.wait_ge(dma_masks, 16)
            dve.tensor_copy(masks_b[:, :, :], masks_sb[:, P:3 * P].rearrange("p (a n) -> p a n", a=2)).then_inc(masks_ready, 1)
            scores_shift(0)
            dve.wait_ge(dma_small, 16 * 3)
            dve.tensor_reduce(gmax[:, :], g1B[:, :], AX.X, ALU.max, apply_absolute_value=True).then_inc(small_ready, 1)
            e_parts(0)
            dve.scalar_tensor_tensor(scr[:, 0], be1_st, 1.0, be1_st, ALU.mult, ALU.mult,
                                     accum_out=norm2[:, 2:3]).then_inc(small_ready, 1)
            dve.wait_ge(dma_wfc, 16)
            dve.tensor_reduce(wfcF[:, :, 0], wfc_st.rearrange("p c (j k) -> p c k j", k=DEPTH), AX.X,
                              ALU.add).then_inc(wfcF_ready, 1)
            dve.wait_ge(wfcF_ready, 1)
            dve.tensor_copy(wfcF[:, :, 1], wfcF[:, :, 0]).then_inc(wfcF_ready, 1)
            xbar_out(0)
            dve.wait_ge(w1_squares, 5)
            dve.tensor_reduce(sq[:, 0:1], sqp[:, 0:4], AX.X, ALU.add).then_inc(bound_ready, 1)
            dve.wait_ge(bound_ready, 1)
            dve.tensor_copy(sq[:, 1:2], sqp[:, 8:9]).then_inc(squares_ready, 1)
            head_rows(0)
            dve.wait_ge(dma_rows, 16 * 3)
            dve.tensor_tensor(addB[:, :], be1_st, b2_st, ALU.add).then_inc(addB_ready, 1)
            dve.wait_ge(norm_ready, 1)
            dve.tensor_copy(bnd[:, 0:1], norm[:, 0:1]).then_inc(bound_ready, 1)
            dve.scalar_tensor_tensor(bnd[:, 1:2], gmax[:, :], 23.0, norm[:, 2:3], ALU.mult, ALU.add).then_inc(bound_ready, 1)
            dve.wait_ge(bound_ready, 3)
            dve.tensor_tensor(bnd[:, 4:5], bnd[:, 1:2], norm[:, 0:1], ALU.mult).then_inc(bound_ready, 1)
            dve.wait_ge(bound_ready, 4)
            dve.tensor_tensor(bnd[:, 2:3], bnd[:, 4:5], norm[:, 1:2], ALU.add).then_inc(bound_ready, 1)
            dve.wait_ge(bound_ready, 5)
            then = power_of_two(slice(0, 3), 0)
            then(dve.tensor_tensor(cc[:, 0:1], isc[:, 0:1], isc[:, 1:2], ALU.mult))
            then(dve.tensor_tensor(c1, cc[:, 0:1], sc[:, 2:3], ALU.mult))
            then(dve.tensor_scalar(b1S, cols[:, 0:NJ], sc[:, 2:3], None, ALU.mult))
            then(dve.tensor_scalar(colsS[:, NJ:], cols[:, NJ:], sc[:, 1:2], None, ALU.mult))
            dve.tensor_copy(cc[:, 3:4], sc[:, 0:1]).then_inc(scales_ready, 1)
            add_attention(0, 0)
            stats(0, 0, yz, y_ready, bn_ready, mv_ready)
            low_w1(0)
            normalise(0)
            dve.wait_ge(dma_w2[3], 16)
            dve.wait_ge(wfc_ready, 1)
            dve.scalar_tensor_tensor(scr[:, :, :].rearrange("p a n -> p (a n)").bitcast(bf16).rearrange(
                "p (c n) -> p c n", c=NC), w2_st[3], 1.0, w2_st[3], ALU.mult, ALU.mult,
                accum_out=sqp[:, 7:8]).then_inc(w2_last_squares, 1)
            dve.wait_ge(w2_squares, 3)
            dve.wait_ge(w2_last_squares, 1)
            dve.tensor_reduce(sq[:, 2:3], sqp[:, 4:8], AX.X, ALU.add).then_inc(squares_ready, 1)
            o1_low(0, 0, 0)
            o1_low(0, 0, 1)
            dve.wait_ge(norm_w2, 1)
            dve.tensor_copy(bnd[:, 3:4], norm[:, 3:4]).then_inc(bound_ready, 1)
            dve.wait_ge(bound_ready, 6)
            then = power_of_two(slice(3, 4), 9)
            then(dve.tensor_tensor(c2, isc[:, 2:3], isc[:, 3:4], ALU.mult))
            dve.tensor_copy(cc[:, 3:4], sc[:, 3:4]).then_inc(w2_scale, 1)
            o1_low(0, 0, 2)
            o1_low(0, 0, 3)
            low_w1(1)
            low_w2(0)
            hidden_low(0, 0)

            R_AT = [0, 4, 11, 14, 21, 25, 32]
            R_AT_FIRST = [0, 8, 13, 17, 23, 26, 29, 32]

            def block_steps(b, slot, front):
                n, nslot = b + 1, 1 - slot
                first = isinstance(b, int) and b == 0
                last = not first
                r_at = R_AT_FIRST if first else R_AT
                for j in range(NJ):
                    if front and j == 7 + first:
                        xbar_out(n)
                    if front and j == 8 + first:
                        head_rows(n)
                    if front and j == 9 + first:
                        add_attention(n, nslot)
                    if front or j < NJ - 1:
                        hidden_low(NJ * b + j + 1, (j + 1) % 2)
                    if last:
                        if j == 6:
                            stats(b - 1, 1, y2, y2_ready, bn2_ready, mv2_ready)
                        if j == 7:
                            ln2(b - 1, (0, 1))
                        if j == 8:
                            ln2(b - 1, (2, 3))
                    if not front:
                        continue
                    if j == 2:
                        x_rest(n, nslot)
                    if j == 4:
                        x_part3(n)
                    if j < 6 + first:
                        scores(n, nslot, r_at[j], r_at[j + 1])
                    if j == 5 + first:
                        scores_max(n, None)
                        scores_shift(n)
                        e_parts(n)
                    if first:
                        if j == 1:
                            low_w2(1)
                        if j in (5, 6):
                            low_w1(j - 3)
                        if j in (7, 9):
                            low_w2((j - 3) // 2)
                    if j == 10:
                        stats(n, 0, yz, y_ready, bn_ready, mv_ready)
                    if j == 11:
                        normalise(n)
                    if j in Z_AT:
                        for c in Z_AT[j]:
                            o1_low(n, nslot, c)
                    if j >= 12:
                        residual(n, nslot, (j - 12,))
                if front:
                    add_ffn(b, slot)

            def last_out(b, slot):
                dve.wait_ge(o1b_ready, NT * (b + 1))
                dve.wait_ge(dma_out, 16 * b)
                for t in range(NT):
                    dve.wait_ge(last_acc_done, t + 1)
                    dve.scalar_tensor_tensor(y2[:, t], acc[t][:, :], c2, o1b[:, slot, t],
                                             ALU.mult, ALU.add).then_inc(y2_ready, 1)
                    dve.wait_ge(y2_ready, NT * b + t + 1)
                    dve.bn_stats(bn[:, 1, t], y2[:, t]).then_inc(bn2_ready, 1)
                    dve.wait_ge(bn2_ready, NT * b + t + 1)
                    dve.bn_aggr(mv[:, 1, t], bn[:, 1, t]).then_inc(mv2_ready, 1)
                for t in range(NT):
                    dve.wait_ge(mv2_ready, NT * b + t + 1)
                    dve.scalar_tensor_tensor(y2[:, t], y2[:, t], mv[:, 1, t, 0:1], g2B[:, :],
                                             ALU.subtract, ALU.mult).then_inc(z2g_ready, 1)
                    dve.wait_ge(rstd_ready[1], b + t + 1)
                    dve.wait_ge(z2g_ready, NT * b + t + 1)
                    dve.scalar_tensor_tensor(y2[:, t], y2[:, t], rstd[:, 1, t:t + 1], be2B[:, :],
                                             ALU.mult, ALU.add).then_inc(out_ready, 1)

            block_steps(0, 0, True)
            with nc.vector.Fori(0, NB // 2 - 1) as i:
                for k in range(2):
                    block_steps(2 * i + 1 + k, 1 - k, True)
            block_steps(NB - 1, 1, False)
            last_out(NB - 1, 1)

        @block.tensor
        def _(te):
            def weighted_x(n):
                te.wait_ge(e_split, 3 * (n + 1))
                te.wait_ge(e1_ready, n + 1)
                te.wait_ge(x1_ready, n + 1)
                te.wait_ge(x2_ready, n + 1)
                te.wait_ge(x3_ready, n + 1)
                if not isinstance(n, int) or n > 0:
                    te.wait_ge(o1f_ready, NC * n - 1)
                W = NP * NH
                for c in range(NC):
                    for t in range(NT):
                        for g in range(NP):
                            w = (NP - g) * NH
                            te.matmul(aux[0][:, c * W:c * W + w], xp[:, g, t, c * P:(c + 1) * P],
                                      ep[:, t, 0:NP - g].rearrange("p g h -> p (g h)"),
                                      start=(t == 0 and g == 0), stop=(t == NT - 1 and g == NP - 1))
                for k in range(2):
                    for t in range(NT):
                        mm = te.matmul(aux[0][:, (NC + k) * W:(NC + k + 1) * W], masks_b[:, k],
                                       ep[:, t].rearrange("p g h -> p (g h)"), start=(t == 0), stop=(t == NT - 1))
                mm.then_inc(xbar_done, 1)

            def project_q(n, slot):
                te.wait_ge(xs_split, 5 * (n + 1))
                if not isinstance(n, int) or n > 0:
                    te.wait_ge(o1f_ready, NC * n)
                W = NP * NH
                for m in range(NC):
                    rows = slice(m * P, (m + 1) * P)
                    for g in range(NP):
                        w = (NP - g) * NH
                        for c in range(NC):
                            te.matmul(aux[1][:, m * W:m * W + w], wqp[:, g, c, rows],
                                      xsp[:, c, 0:NP - g].rearrange("p g h -> p (g h)"),
                                      start=(c == 0 and g == 0), stop=False)
                        mm = te.matmul(aux[1][:, m * W:m * W + w], peb[:, slot, g, rows],
                                       xsp[0:SPB, NC + 1, 0:NP - g].rearrange("p g h -> p (g h)"),
                                       start=False, stop=(g == NP - 1))
                mm.then_inc(o_done, 1)

            def project_out(n):
                te.wait_ge(ocx_ready, 2 * (n + 1))
                te.wait_ge(xs_ready, n + 1)
                te.matmul(aux[0][:, :], ocx[:, :, :].rearrange("p h r -> p (h r)"), wfcS[:, :],
                          start=True, stop=True).then_inc(ao_done, 1)

            def transpose_z(n, c):
                te.wait_ge(z_ready, NT * (n + 1))
                if c >= 2:
                    te.wait_ge(o1f_ready, NC * n + c - 1)
                for t in range(NT):
                    mm = te.transpose(aux[c % 2][:, t * P:(t + 1) * P], yz[:, t, c * P:(c + 1) * P], ident)
                mm.then_inc(zT_done, 1)

            def ffn1(g, j, slot):
                s = j % 2
                if not isinstance(g, int) or g >= 2:
                    te.wait_ge(hf_ready, g - 1)
                k = 0
                for c in range(NC):
                    if isinstance(g, int) and g == 0:
                        te.wait_ge(o1hi_ready, c + 1)
                        te.wait_ge(o1lo_ready, c + 1)
                    cols_ = slice(j * P, (j + 1) * P)
                    for w, o in ((w1hi, o1hi), (w1hi, o1lo), (w1lo, o1hi)):
                        mm = te.matmul(hps[s][:, :], w[:, c, cols_], o[:, slot, c],
                                       start=(k == 0), stop=(k == 3 * NC - 1))
                        k += 1
                mm.then_inc(ffn1_done, 1)

            def ffn2(g, j, b):
                s = j % 2
                te.wait_ge(hhi_ready, g + 1)
                for t in range(NT):
                    if j == 0 and (not isinstance(b, int) or b > 0):
                        te.wait_ge(y2_ready, NT * (b - 1) + t + 1)
                    tok = slice(t * P, (t + 1) * P)
                    te.matmul(acc[t][:, :], hhi[:, s, tok], w2hi[:, j], start=(j == 0), stop=False)
                    te.matmul(acc[t][:, :], hhi[:, s, tok], w2lo[:, j], start=False, stop=False)
                te.wait_ge(hlo_ready, g + 1)
                for t in range(NT):
                    tok = slice(t * P, (t + 1) * P)
                    mm = te.matmul(acc[t][:, :], hlo[:, s, tok], w2hi[:, j], start=False, stop=(j == NJ - 1))
                mm.then_inc(ffn2_done, 1)

            def spread_wr(h):
                if h >= 5:
                    te.wait_ge(wrB_ready, h - 4)
                for c in range(NC):
                    mm = te.transpose(wr_banks[h][:, c * P:(c + 1) * P], wr_c[:, c, h:h + 1].broadcast_to([P, P]), ident)
                mm.then_inc(wr_ready, 1)

            te.wait_ge(dma_masks, 16)
            te.wait_ge(dma_x[0], 32)
            for c in range(NC):
                for t in range(NT):
                    mm = te.transpose(acc[c][:, t * P:(t + 1) * P], xb[:, 0, t, c * P:(c + 1) * P], ident)
                mm.then_inc(xT_done, 1)
            te.wait_ge(wrc_ready, 1)
            te.wait_ge(xT_ready, NC)
            for t in range(NT):
                for c in range(NC):
                    mm = te.matmul(aux[1][:, t * NH:(t + 1) * NH], xT_st[:, c, t * P:(t + 1) * P], wr_c[:, c],
                                   start=(c == 0), stop=(c == NC - 1))
            mm.then_inc(r0_done, 1)
            for h in range(4):
                spread_wr(h)
            te.wait_ge(masks_ready, 1)
            weighted_x(0)
            te.wait_ge(wfcF_ready, 2)
            for c in range(NC):
                mm = te.transpose(acc[3][:, c * P:(c + 1) * P], wfcF[:, c].rearrange("p a k -> p (a k)"), ident)
            mm.then_inc(wfc_ready, 1)
            te.wait_ge(wq_split, 4)
            te.wait_ge(rmx_ready, 1)
            project_q(0, 0)
            spread_wr(4)
            spread_wr(5)
            te.wait_ge(wfcS_ready, 1)
            project_out(0)
            spread_wr(6)
            spread_wr(7)
            for c in range(NC):
                transpose_z(0, c)
            te.wait_ge(w1lo_ready, 1)
            te.wait_ge(wrB_ready, NH)
            ffn1(0, 0, 0)

            def ffn2_last(g, j):
                s = j % 2
                te.wait_ge(hhi_ready, g + 1)
                te.wait_ge(hlo_ready, g + 1)
                for t in range(NT):
                    tok = slice(t * P, (t + 1) * P)
                    te.matmul(acc[t][:, :], hhi[:, s, tok], w2hi[:, j], start=False, stop=False)
                    te.matmul(acc[t][:, :], hhi[:, s, tok], w2lo[:, j], start=False, stop=False)
                    te.matmul(acc[t][:, :], hlo[:, s, tok], w2hi[:, j], start=False, stop=True).then_inc(last_acc_done, 1)

            def block_steps(b, slot, front):
                n, nslot = b + 1, 1 - slot
                first = isinstance(b, int) and b == 0
                for j in range(NJ):
                    if front and j == NJ - 1:
                        te.wait_ge(o1hi_ready, NC * (n + 1))
                        te.wait_ge(o1lo_ready, NC * (n + 1))
                        ffn1(NJ * n, 0, nslot)
                    if j < NJ - 1:
                        if first and (j + 1) % 4 == 0:
                            te.wait_ge(w1lo_ready, (j + 1) // 4 + 1)
                        ffn1(NJ * b + j + 1, j + 1, slot)
                    if front and j == 7 + first:
                        weighted_x(n)
                    if front and j == 8 + first:
                        project_q(n, nslot)
                    if front and j == 9 + first:
                        project_out(n)
                    if front and j in Z_AT:
                        for c in Z_AT[j]:
                            transpose_z(n, c)
                    if first and j % 4 == 0:
                        te.wait_ge(w2lo_ready, j // 4 + 1)
                    if not front and j == NJ - 1:
                        ffn2_last(NJ * b + j, j)
                    else:
                        ffn2(NJ * b + j, j, b)

            block_steps(0, 0, True)
            with nc.tensor.Fori(0, NB // 2 - 1) as i:
                for k in range(2):
                    block_steps(2 * i + 1 + k, 1 - k, True)
            block_steps(NB - 1, 1, False)


def kernel(x, L0_conv_Wq, L0_conv_Wfc, L0_conv_W1, L0_conv_b1, L0_conv_W2, L0_conv_b2,
           L0_conv_g1, L0_conv_be1, L0_conv_g2, L0_conv_be2):
    import numpy as np
    import concourse.bacc as bacc
    from concourse.bass_utils import run_bass_kernel_spmd

    S = x.shape[0]
    pos = np.arange(S, dtype=np.float32)[:, None]
    div = np.exp(np.arange(0, D, 2, dtype=np.float32) * np.float32(-np.log(10000.0) / D)).astype(np.float32)
    ang = (pos * div).astype(np.float32)
    pe = np.zeros((S, D), np.float32)
    pe[:, 0::2] = np.sin(ang)
    pe[:, 1::2] = np.cos(ang)
    parts, rest = [], pe
    for _ in range(NP):
        cut = (rest.view(np.uint32) & np.uint32(0xFFFF0000)).view(np.float32)
        parts.append((cut.view(np.uint32) >> 16).astype(np.uint16))
        rest = rest - cut
    pr = pe.reshape(NB, SPB, NH, DEPTH).sum(-1, dtype=np.float64).astype(np.float32)
    p = np.arange(P)
    pe_r = np.ascontiguousarray(pr[:, p // 4, :].transpose(1, 0, 2).reshape(P, NB * NH))
    masks = np.concatenate([np.eye(P), np.ones((P, P)),
                            (p[:, None] // 4 == p[None, :])], axis=1).astype(np.float32)
    cols = np.ascontiguousarray(np.concatenate(
        [np.asarray(v).reshape(-1, P) for v in (L0_conv_b1, L0_conv_g1, L0_conv_be1)], axis=0).T)
    arrays = {
        "x": np.ascontiguousarray(x).reshape(-1, D),
        "wqT": np.ascontiguousarray(np.asarray(L0_conv_Wq).T),
        "wfc": np.ascontiguousarray(L0_conv_Wfc),
        "w1T": np.ascontiguousarray(np.asarray(L0_conv_W1).T),
        "w2T": np.ascontiguousarray(np.asarray(L0_conv_W2).T),
        "b2": np.ascontiguousarray(L0_conv_b2),
        "g1": np.ascontiguousarray(L0_conv_g1),
        "be1": np.ascontiguousarray(L0_conv_be1),
        "g2": np.ascontiguousarray(L0_conv_g2),
        "be2": np.ascontiguousarray(L0_conv_be2),
        "cols": cols,
        "pe_parts": np.ascontiguousarray(np.stack(parts, axis=1)),
        "pe_r": pe_r,
        "masks": masks,
    }
    nc = bacc.Bacc("TRN2", target_bir_lowering=False, num_devices=1)
    args = [nc.dram_tensor(f"in_{k}", a.shape, mybir.dt.from_np(a.dtype), kind="ExternalInput").ap() for k, a in arrays.items()]
    out = nc.dram_tensor("out_y", (NB * TB, D), mybir.dt.float32, kind="ExternalOutput").ap()
    conv_seq_kernel(nc, *args, out)
    r = run_bass_kernel_spmd(nc, [{f"in_{k}": a for k, a in arrays.items()}], core_ids=[0])
    return r.results[0]["out_y"].reshape(x.shape)
```
